# Optimizing a Trainium2 kernel written in Bass

```python
import numpy as np
import jax
import jax.numpy as jnp

def _softmax(x, axis=-1):
    return jax.nn.softmax(x, axis=axis)

def _gelu(x):
    return jax.nn.gelu(x, approximate=True)

def _silu(x):
    return jax.nn.silu(x)

def _sigmoid(x):
    return jax.nn.sigmoid(x)

def _layernorm(x, axis=-1, eps=1e-05):
    m = jnp.mean(x, axis=axis, keepdims=True)
    v = jnp.var(x, axis=axis, keepdims=True)
    return (x - m) / jnp.sqrt(v + eps)

def _scatter_add(tgt, idx, src, axis=0):
    return tgt.at[idx].add(src)

def _segment_sum(src, seg, n):
    return jax.ops.segment_sum(src, seg, n)
kernel_name = 'mk_audio_tower_d1_tok_audfeat256_r4_f00f58'

def setup_inputs(seed: int=0):
    np.random.seed(seed)
    _w = jnp.asarray

    def _rec_inputs():
        import jax
        import jax.numpy as jnp
        _rk = jax.random.key(seed)
        x = jax.random.uniform(jax.random.fold_in(_rk, 1), (8, 4, 750), jnp.float32, 0.0, 0.999986)
        return x
    x = _rec_inputs()

    def _L0_tok_setup():
        import jax, jax.numpy as jnp
        import numpy as np
        T = 8
        key = jax.random.key(seed)
        ks = jax.random.split(key, 9)
        bs, dims, L, d = (16, 4, 512, 64)
        x = jax.random.uniform(ks[0], (bs, dims, L), dtype=jnp.float32)
        s_in = 1.0 / np.sqrt(dims)
        s_d = 1.0 / np.sqrt(d)
        W1 = jax.random.uniform(ks[1], (d, dims), minval=-s_in, maxval=s_in, dtype=jnp.float32)
        b1 = jax.random.uniform(ks[2], (d,), minval=-s_in, maxval=s_in, dtype=jnp.float32)
        W2 = jax.random.uniform(ks[3], (d, d), minval=-s_d, maxval=s_d, dtype=jnp.float32)
        b2 = jax.random.uniform(ks[4], (d,), minval=-s_d, maxval=s_d, dtype=jnp.float32)
        W3 = jax.random.uniform(ks[5], (d, dims), minval=-s_in, maxval=s_in, dtype=jnp.float32)
        b3 = jax.random.uniform(ks[6], (d,), minval=-s_in, maxval=s_in, dtype=jnp.float32)
        W4 = jax.random.uniform(ks[7], (d, d), minval=-s_d, maxval=s_d, dtype=jnp.float32)
        b4 = jax.random.uniform(ks[8], (d,), minval=-s_d, maxval=s_d, dtype=jnp.float32)
        return dict(x=x, W1=W1, b1=b1, W2=W2, b2=b2, W3=W3, b3=b3, W4=W4, b4=b4)
    _L0_tok_all = _L0_tok_setup()
    _L0_tok_in = {k: v for k, v in _L0_tok_all.items() if k in ('W1', 'b1', 'W2', 'b2', 'W3', 'b3', 'W4', 'b4')}
    del _L0_tok_all

    def _L0_attn_setup():
        import jax, jax.numpy as jnp
        import numpy as np
        D_MODEL = 64
        N_HEAD = 8

        def _l1_scores(q, k):
            scale = 1.0 / np.sqrt(q.shape[-1]).astype(np.float32)
            q_sbhw = q.transpose(1, 0, 2, 3)

            def one_query(qs):
                return -jnp.sum(jnp.abs(qs[:, None, :, :] - k), axis=-1) * scale
            s = jax.lax.map(one_query, q_sbhw)
            return s.transpose(1, 0, 2, 3)
        key = jax.random.key(seed)
        ks = jax.random.split(key, 3)
        b, t = (4, 250)
        x = jax.random.normal(ks[0], (b, t, D_MODEL), jnp.float32)
        wqv_w = 0.005 * jax.random.normal(ks[1], (3 * N_HEAD * D_MODEL, D_MODEL), jnp.float32)
        wqv_b = jnp.zeros((3 * N_HEAD * D_MODEL,), jnp.float32)
        wk = 0.005 * jnp.ones((N_HEAD, D_MODEL), jnp.float32)
        fanin_w = 0.005 * jax.random.normal(ks[2], (D_MODEL, D_MODEL), jnp.float32)
        fanin_b = jnp.zeros((D_MODEL,), jnp.float32)
        return dict(x=x, wqv_w=wqv_w, wqv_b=wqv_b, wk=wk, fanin_w=fanin_w, fanin_b=fanin_b)
    _L0_attn_all = _L0_attn_setup()
    _L0_attn_in = {k: v for k, v in _L0_attn_all.items() if k in ('wqv_w', 'wqv_b', 'wk', 'fanin_w', 'fanin_b')}
    del _L0_attn_all

    def _L0_ffn_setup():
        import jax, jax.numpy as jnp
        import numpy as np
        B, S, D, H, E, K = (8, 2048, 64, 256, 8, 2)
        key = jax.random.key(seed)
        ks = jax.random.split(key, 7)
        s_in = 1.0 / np.sqrt(D)
        s_hid = 1.0 / np.sqrt(H)
        return {'x': jax.random.normal(ks[0], (B, S, D), dtype=jnp.float32), 'Wg': jax.random.uniform(ks[1], (E, D), jnp.float32, -s_in, s_in), 'bg': jax.random.uniform(ks[2], (E,), jnp.float32, -s_in, s_in), 'W1': jax.random.uniform(ks[3], (E, H, D), jnp.float32, -s_in, s_in), 'b1': jax.random.uniform(ks[4], (E, H), jnp.float32, -s_in, s_in), 'W2': jax.random.uniform(ks[5], (E, D, H), jnp.float32, -s_hid, s_hid), 'b2': jax.random.uniform(ks[6], (E, D), jnp.float32, -s_hid, s_hid)}
    _L0_ffn_all = _L0_ffn_setup()
    _L0_ffn_in = {k: v for k, v in _L0_ffn_all.items() if k in ('Wg', 'bg', 'W1', 'b1', 'W2', 'b2')}
    del _L0_ffn_all
    return {'x': x, 'L0_tok_W1': _L0_tok_in['W1'], 'L0_tok_b1': _L0_tok_in['b1'], 'L0_tok_W2': _L0_tok_in['W2'], 'L0_tok_b2': _L0_tok_in['b2'], 'L0_tok_W3': _L0_tok_in['W3'], 'L0_tok_b3': _L0_tok_in['b3'], 'L0_tok_W4': _L0_tok_in['W4'], 'L0_tok_b4': _L0_tok_in['b4'], 'L0_attn_wqv_w': _L0_attn_in['wqv_w'], 'L0_attn_wqv_b': _L0_attn_in['wqv_b'], 'L0_attn_wk': _L0_attn_in['wk'], 'L0_attn_fanin_w': _L0_attn_in['fanin_w'], 'L0_attn_fanin_b': _L0_attn_in['fanin_b'], 'L0_ffn_Wg': _L0_ffn_in['Wg'], 'L0_ffn_bg': _L0_ffn_in['bg'], 'L0_ffn_W1': _L0_ffn_in['W1'], 'L0_ffn_b1': _L0_ffn_in['b1'], 'L0_ffn_W2': _L0_ffn_in['W2'], 'L0_ffn_b2': _L0_ffn_in['b2']}

def reference(x, L0_tok_W1, L0_tok_b1, L0_tok_W2, L0_tok_b2, L0_tok_W3, L0_tok_b3, L0_tok_W4, L0_tok_b4, L0_attn_wqv_w, L0_attn_wqv_b, L0_attn_wk, L0_attn_fanin_w, L0_attn_fanin_b, L0_ffn_Wg, L0_ffn_bg, L0_ffn_W1, L0_ffn_b1, L0_ffn_W2, L0_ffn_b2):
    import jax
    import jax.numpy as jnp

    def _L0_tok_ref(x, W1, b1, W2, b2, W3, b3, W4, b4):
        import jax, jax.numpy as jnp
        import numpy as np
        T = 8
        a = jnp.einsum('bdl,od->blo', x, W1) + b1
        bs, L, d = a.shape
        zcol = jnp.zeros((bs, 1, d), a.dtype)
        shift_r = lambda v: jnp.concatenate([zcol, v[:, :-1]], axis=1)
        shift_l = lambda v: jnp.concatenate([v[:, 1:], zcol], axis=1)
        up = jnp.zeros_like(a)
        down = jnp.zeros_like(a)
        for _ in range(T):
            up = jax.nn.relu(a + shift_r(up) @ W2.T + b2)
            down = jax.nn.relu(a + shift_l(down) @ W2.T + b2)
        c = jnp.einsum('bdl,od->blo', x, W3) + b3
        miu = jax.nn.relu(c + (shift_r(up) @ W4.T + b4) + (shift_l(down) @ W4.T + b4))
        return miu

    def _L0_attn_ref(x, wqv_w, wqv_b, wk, fanin_w, fanin_b):
        import jax, jax.numpy as jnp
        import numpy as np
        D_MODEL = 64
        N_HEAD = 8

        def _l1_scores(q, k):
            scale = 1.0 / np.sqrt(q.shape[-1]).astype(np.float32)
            q_sbhw = q.transpose(1, 0, 2, 3)

            def one_query(qs):
                return -jnp.sum(jnp.abs(qs[:, None, :, :] - k), axis=-1) * scale
            s = jax.lax.map(one_query, q_sbhw)
            return s.transpose(1, 0, 2, 3)
        b, t, d = x.shape
        h = N_HEAD
        v = (x @ wqv_w.T + wqv_b).reshape(b, t, 3 * h, d)
        q, vf, vb = (v[:, :, :h], v[:, :, h:2 * h], v[:, :, 2 * h:])
        k = x[:, :, None, :] * wk[None, None]
        a = _l1_scores(q, k)
        a = jnp.concatenate([a, jnp.zeros((b, 1, t, h), a.dtype)], axis=1)
        a = jax.nn.softmax(a, axis=1)[:, :t]
        bf = jnp.einsum('bsdh,bshw->bdhw', a, vf)
        bb = jnp.einsum('bdsh,bshw->bdhw', a, vb)
        o = (bf + bb).sum(axis=2).reshape(b, t, d)
        y = o * jax.nn.sigmoid(1.702 * o)
        y = y @ fanin_w.T + fanin_b
        return x + y

    def _L0_ffn_ref(x, Wg, bg, W1, b1, W2, b2):
        import jax, jax.numpy as jnp
        import numpy as np
        B, S, D, H, E, K = (8, 2048, 64, 256, 8, 2)
        gate_scores = jnp.einsum('bsd,ed->bse', x, Wg) + bg
        topk_scores, topk_idx = jax.lax.top_k(gate_scores, K)
        topk_probs = jax.nn.softmax(topk_scores, axis=-1)
        combine = jnp.sum(topk_probs[..., None] * jax.nn.one_hot(topk_idx, E, dtype=x.dtype), axis=-2)
        out = jnp.zeros_like(x)
        for e in range(E):
            h = jax.nn.relu(jnp.einsum('bsd,hd->bsh', x, W1[e]) + b1[e])
            y = jnp.einsum('bsh,dh->bsd', h, W2[e]) + b2[e]
            out = out + combine[..., e:e + 1] * y
        return out
    h = _L0_tok_ref(x, L0_tok_W1, L0_tok_b1, L0_tok_W2, L0_tok_b2, L0_tok_W3, L0_tok_b3, L0_tok_W4, L0_tok_b4)
    h = h + _L0_attn_ref(_layernorm(h, axis=-1), L0_attn_wqv_w, L0_attn_wqv_b, L0_attn_wk, L0_attn_fanin_w, L0_attn_fanin_b)
    h = h + _L0_ffn_ref(_layernorm(h, axis=-1), L0_ffn_Wg, L0_ffn_bg, L0_ffn_W1, L0_ffn_b1, L0_ffn_W2, L0_ffn_b2)
    return h

_drawn_inputs = setup_inputs


def setup_inputs(seed=0):
    import zlib

    import numpy as np

    out = dict(_drawn_inputs(seed))
    spreads = {'L0_attn_wqv_b': (0.0, 0.8),
     'L0_attn_wk': (0.004999999888241291, 0.6),
     'L0_attn_fanin_b': (0.0, 0.1)}
    factors = {'L0_attn_wqv_w': 8.0, 'L0_attn_fanin_w': 7.112, 'L0_ffn_b1': 4.009, 'L0_ffn_b2': 3.09}
    for name, (base, spread) in spreads.items():
        noise = np.random.default_rng([zlib.crc32(name.encode()), seed]).standard_normal(out[name].shape)
        drawn = base * np.exp(spread * noise) if base else spread * noise
        out[name] = jnp.asarray(drawn.astype(out[name].dtype))
    for name, factor in factors.items():
        out[name] = (out[name] * factor).astype(out[name].dtype)
    return out
```

```python
import concourse.bass as bass
from concourse import mybir
from contextlib import ExitStack

F32 = mybir.dt.float32
BF16 = mybir.dt.bfloat16
ALU = mybir.AluOpType
ACT = mybir.ActivationFunctionType
AX = mybir.AxisListType

B, DIMS, L, D = 8, 4, 750, 64
TOK = B * L
ROUNDS = 8
HALF = L // 2
CH = 125
NC = TOK // CH
BC = L // CH
NH = 8
HP = NH // 2
NE, HID = 8, 256
EPS = 1e-5
QUADS = 4
ROWS = 16
TILE = QUADS * ROWS
FULL = L // TILE
LASTN = L - FULL * TILE
LROWS = -(-LASTN // QUADS)
NT = FULL + 1
STEPS = FULL * ROWS + LROWS
RING = 4
SCALAR_SHARE = (1, 2, 2, 1, 2, 2, 1, 2)
VC = D + 1
VCH = 120
EC = 500


def reversed_half(buf, b):
    a = buf[64:128, b, L - 1:L]
    return bass.AP(a.tensor, a.offset, [list(a.ap[0]), [-HALF, 2], [-1, HALF]])


def on_scalar(i, j):
    return j < SCALAR_SHARE[i % len(SCALAR_SHARE)]


def build(nc, A, out):
    scratch_qk = nc.dram_tensor("scratch_qk", (B * HP, 128, 3 * L), F32, kind="Internal").ap()
    scratch_ks = nc.dram_tensor("scratch_ks", (NH * 3, TOK), BF16, kind="Internal").ap()
    scratch_v = nc.dram_tensor("scratch_v", (TOK, 2 * NH * D), F32, kind="Internal").ap()

    whole = ExitStack()
    with whole:
        def sbuf(ctx, name, shape, dt=F32):
            return ctx.enter_context(nc.sbuf_tensor(name, shape, dt))

        def psum(ctx, name, shape):
            return ctx.enter_context(nc.psum_tensor(name, shape, F32))

        def semaphore(ctx, name):
            return ctx.enter_context(nc.semaphore(name))

        hx = sbuf(whole, "hx", [CH, NC, D])
        of_acc = sbuf(whole, "of_acc", [CH, BC + NC, D])
        ob_acc = sbuf(whole, "ob_acc", [128, 1 + B, HALF])
        ident = sbuf(whole, "ident", [128, 128])
        window = sbuf(whole, "window", [128, 62])
        select = sbuf(whole, "select", [6, 2, 128], BF16)
        vinit = sbuf(whole, "vinit", [128, 4])

        phase_tokens(nc, A, sbuf, psum, semaphore, hx, of_acc, ob_acc, ident, window, select, vinit,
                     scratch_qk, scratch_ks, scratch_v)
        phase_attend(nc, sbuf, psum, semaphore, of_acc, ob_acc, ident, window, select, vinit,
                     scratch_qk, scratch_ks, scratch_v)
        phase_feed(nc, A, out, sbuf, psum, semaphore, hx, of_acc, ob_acc, ident)


def layernorm(nc, vec, link, src, mean, var, cen, sq, var_ready, std_ready, level):
    n, c = src.shape[0], src.shape[1]
    link(vec.reduce_sum(mean[:, :], src, axis=AX.X))
    link(vec.tensor_scalar(mean[:, :], mean[:, :], 1.0 / D, None, ALU.mult))
    link(vec.tensor_tensor(cen, src, mean[:, :].unsqueeze(2).to_broadcast([n, c, D]), ALU.subtract))
    link(vec.tensor_tensor(sq, cen, cen, ALU.mult))
    link(vec.reduce_sum(var[:, :], sq, axis=AX.X))
    vec.tensor_scalar(var[:, :], var[:, :], 1.0 / D, EPS, ALU.mult, ALU.add).then_inc(var_ready, 1)
    vec.wait_ge(std_ready, level)
    link(vec.reciprocal(var[:, :], var[:, :]))


def phase_tokens(nc, A, sbuf, psum, semaphore, hx, of_acc, ob_acc, ident, window, select, vinit,
                 scratch_qk, scratch_ks, scratch_v):
    with ExitStack() as ctx:
        h1 = sbuf(ctx, "h1", [CH, NC, D])
        w1b = sbuf(ctx, "w1b", [10, 128])
        w2b = sbuf(ctx, "w2b", [128, 128])
        w4d = sbuf(ctx, "w4d", [128, D])
        w3b = sbuf(ctx, "w3b", [7, D])
        select32 = sbuf(ctx, "select32", [6, 2, 128])
        with ExitStack() as inner:
            x10 = sbuf(inner, "x10", [10, B, L])
            x7 = sbuf(inner, "x7", [7, TOK])
            state = sbuf(inner, "state", [128, B, L + 2])
            last = sbuf(inner, "last", [128, B, L + 2])
            ps = [psum(inner, f"ps{k}", [128, 2, 512]) for k in range(4)]
            loaded = semaphore(inner, "loaded")
            zeroed = semaphore(inner, "zeroed")
            summed = semaphore(inner, "summed")
            kept_act = semaphore(inner, "kept_act")
            kept_vec = semaphore(inner, "kept_vec")
            mixed = semaphore(inner, "mixed")
            mixed_act = semaphore(inner, "mixed_act")
            mixed_vec = semaphore(inner, "mixed_vec")
            NLOAD = 10
            with nc.Block() as block:
                @block.sync
                def _(sp):
                    sp.dma_start(x10[:, :, :], A["x10"].rearrange("k (b l) -> k b l", b=B)).then_inc(loaded, 16)
                    sp.dma_start(w1b[:, :], A["w1b"]).then_inc(loaded, 16)
                    sp.dma_start(w2b[:, :], A["w2b"]).then_inc(loaded, 16)
                    sp.dma_start(w4d[:, :], A["w4d"]).then_inc(loaded, 16)
                    sp.dma_start(w3b[:, :], A["w3b"]).then_inc(loaded, 16)
                    sp.dma_start(x7[:, :], A["x7"]).then_inc(loaded, 16)
                    sp.dma_start(ident[:, :], A["ident"]).then_inc(loaded, 16)
                    sp.dma_start(window[:, :], A["window"]).then_inc(loaded, 16)
                    sp.dma_start(select32[:, :, :], A["select"].rearrange("r (a p) -> r a p", a=2)).then_inc(loaded, 16)
                    sp.dma_start(vinit[:, :], A["vinit"]).then_inc(loaded, 16)
                    sp.wait_ge(loaded, 16 * NLOAD)

                @block.gpsimd
                def _(pool):
                    pool.memset(state[:, :, 0:1], 0.0).then_inc(zeroed, 1)
                    pool.memset(last[:, :, 1:2], 0.0).then_inc(zeroed, 1)
                    pool.memset(last[:, :, L:L + 1], 0.0).then_inc(zeroed, 1)
                    pool.memset(of_acc[:, :, :], 0.0)
                    pool.memset(ob_acc[:, :, :], 0.0)

                @block.tensor
                def _(pe):
                    pe.wait_ge(loaded, 16 * NLOAD)
                    pe.wait_ge(zeroed, 3)

                    def into(b, h):
                        return ps[b % 4][:, h, 0:HALF]

                    for b in range(B):
                        if b >= 4:
                            pe.wait_ge((kept_act, kept_vec)[b % 2], (b - 4) // 2 + 1)
                        for h in range(2):
                            mm = pe.matmul(into(b, h), w1b[:, :], x10[:, b, h * HALF:(h + 1) * HALF],
                                           start=True, stop=True)
                        mm.then_inc(summed, 1)
                    with pe.Fori(1, ROUNDS) as t:
                        for b in range(B):
                            pe.wait_ge((kept_act, kept_vec)[b % 2], t * 4 + (b // 2 - 1))
                            for h in range(2):
                                pe.matmul(into(b, h), w1b[:, :], x10[:, b, h * HALF:(h + 1) * HALF],
                                          start=True, stop=False)
                                mm = pe.matmul(into(b, h), w2b[:, :], state[:, b, h * HALF:(h + 1) * HALF],
                                               start=False, stop=True)
                            mm.then_inc(summed, 1)
                    pe.wait_ge(kept_act, 4 * ROUNDS)
                    pe.wait_ge(kept_vec, 4 * ROUNDS)
                    for g in range(NC // 8):
                        for k in range(8):
                            c = 8 * g + k
                            b, o = c // BC, 1 + CH * (c % BC)
                            dst = ps[g // 2][0:CH, g % 2, D * k:D * k + D]
                            pe.matmul(dst, last[:, b, o:o + CH], w4d[:, :], start=True, stop=False)
                            mm = pe.matmul(dst, x7[:, CH * c:CH * c + CH], w3b[:, :], start=False, stop=True)
                        mm.then_inc(mixed, 1)

                def two(buf, lo, p0=0, p1=128):
                    return lambda b: buf[p0:p1, b, lo:lo + L].rearrange("p (h c) -> p h c", h=2)

                @block.scalar
                def _(act):
                    act.wait_ge(zeroed, 3)
                    for b in range(0, B, 2):
                        act.wait_ge(summed, b + 1)
                        act.activation(two(state, 1)(b), ps[b % 4][:, :, 0:HALF], ACT.Relu).then_inc(kept_act, 1)
                    with act.Fori(1, ROUNDS - 1) as t:
                        for b in range(0, B, 2):
                            act.wait_ge(summed, t * B + b + 1)
                            act.activation(two(state, 1)(b), ps[b % 4][:, :, 0:HALF], ACT.Relu).then_inc(kept_act, 1)
                    for b in range(0, B, 2):
                        act.wait_ge(summed, (ROUNDS - 1) * B + b + 1)
                        act.activation(two(last, 2, 0, 64)(b), ps[b % 4][0:64, :, 0:HALF], ACT.Relu)
                        act.activation(reversed_half(last, b), ps[b % 4][64:128, :, 0:HALF],
                                       ACT.Relu).then_inc(kept_act, 1)
                    for g in range(0, NC // 8, 2):
                        act.wait_ge(mixed, g + 1)
                        act.activation(h1[:, 8 * g:8 * g + 8, :], ps[g // 2][0:CH, 0, :].rearrange("p (k d) -> p k d", k=8),
                                       ACT.Relu).then_inc(mixed_act, 1)

                @block.vector
                def _(vec):
                    vec.wait_ge(zeroed, 3)
                    vec.wait_ge(loaded, 16 * NLOAD)
                    vec.tensor_copy(select[:, :, :], select32[:, :, :])
                    for b in range(1, B, 2):
                        vec.wait_ge(summed, b + 1)
                        vec.tensor_scalar(two(state, 1)(b), ps[b % 4][:, :, 0:HALF], 0.0, None, ALU.max).then_inc(kept_vec, 1)
                    with vec.Fori(1, ROUNDS - 1) as t:
                        for b in range(1, B, 2):
                            vec.wait_ge(summed, t * B + b + 1)
                            vec.tensor_scalar(two(state, 1)(b), ps[b % 4][:, :, 0:HALF], 0.0, None,
                                              ALU.max).then_inc(kept_vec, 1)
                    for b in range(1, B, 2):
                        vec.wait_ge(summed, (ROUNDS - 1) * B + b + 1)
                        vec.tensor_scalar(two(last, 2, 0, 64)(b), ps[b % 4][0:64, :, 0:HALF], 0.0, None, ALU.max)
                        vec.tensor_scalar(reversed_half(last, b), ps[b % 4][64:128, :, 0:HALF], 0.0, None,
                                          ALU.max).then_inc(kept_vec, 1)
                    for g in range(1, NC // 8, 2):
                        vec.wait_ge(mixed, g + 1)
                        vec.tensor_scalar(h1[:, 8 * g:8 * g + 8, :],
                                          ps[g // 2][0:CH, 1, :].rearrange("p (k d) -> p k d", k=8),
                                          0.0, None, ALU.max).then_inc(mixed_vec, 1)

        with ExitStack() as inner:
            mean = sbuf(inner, "mean", [CH, NC])
            var = sbuf(inner, "var", [CH, NC])
            cen = sbuf(inner, "cen", [CH, NC, D])
            twice = sbuf(inner, "twice", [CH, NC, 2, D])
            xt = sbuf(inner, "xt", [128, TOK])
            wq = sbuf(inner, "wq", [D, NH * D])
            wv = sbuf(inner, "wv", [D, 2 * NH * D])
            bq = sbuf(inner, "bq", [128, HP])
            bv = sbuf(inner, "bv", [128, 2 * NH * D])
            wkc = sbuf(inner, "wkc", [128, HP])
            wkt = sbuf(inner, "wkt", [D, NH])
            qk = [sbuf(inner, f"qk_out{k}", [128, 3, L]) for k in range(2)]
            vs = [sbuf(inner, f"vs{k}", [VCH, 2 * NH * D]) for k in range(2)]
            xb = [sbuf(inner, f"xb{k}", [D, L]) for k in range(2)]
            ks32 = sbuf(inner, "ks32", [NH, TOK])
            kparts = sbuf(inner, "kparts", [NH, 2, TOK], BF16)
            pt = [psum(inner, f"pt{k}", [128, 512]) for k in range(2)]
            pq = [psum(inner, f"pq{k}", [128, 2, 512]) for k in range(2)]
            pv = [psum(inner, f"pv{k}", [128, 512]) for k in range(2)]
            weights = semaphore(inner, "weights")
            chain = semaphore(inner, "chain_b")
            var_ready = semaphore(inner, "var_ready")
            std_ready = semaphore(inner, "std_ready")
            norm_ready = semaphore(inner, "norm_ready")
            twice_ready = semaphore(inner, "twice_ready")
            turned = semaphore(inner, "turned")
            xt_act = semaphore(inner, "xt_act")
            xt_vec = semaphore(inner, "xt_vec")
            ks_sum = semaphore(inner, "ks_sum")
            ks_kept = semaphore(inner, "ks_kept")
            part_act = semaphore(inner, "part_act")
            part_vec = semaphore(inner, "part_vec")
            q_sum = semaphore(inner, "q_sum")
            q_made = semaphore(inner, "q_made")
            nq_made = semaphore(inner, "nq_made")
            k_made = semaphore(inner, "k_made")
            xb_made = semaphore(inner, "xb_made")
            turn_b = semaphore(inner, "turn_b")
            qk_stored = [semaphore(inner, f"qk_stored{k}") for k in range(2)]
            v_sum = semaphore(inner, "v_sum")
            v_made = semaphore(inner, "v_made")
            v_stored = [semaphore(inner, f"v_stored{k}") for k in range(2)]
            ks_stored = [semaphore(inner, f"ks_stored{k}") for k in range(3)]
            NV = TOK // VCH
            QCRED = 2 * HP + 2
            with nc.Block() as block:
                @block.sync
                def _(sp):
                    sp.dma_start(wq[:, :], A["wq"]).then_inc(weights, 16)
                    sp.dma_start(wv[:, :], A["wv"]).then_inc(weights, 16)
                    sp.dma_start(bq[:, :], A["bq"]).then_inc(weights, 16)
                    sp.dma_start(bv[:, :], A["bv"].partition_broadcast(128)).then_inc(weights, 16)
                    sp.dma_start(wkc[:, :], A["wkc"]).then_inc(weights, 16)
                    sp.dma_start(wkt[:, :], A["wkt"]).then_inc(weights, 16)
                    parts = scratch_ks.rearrange("(h k) t -> h k t", k=3)
                    for k in range(3):
                        sp.wait_ge(part_act, k + 1)
                        sp.dma_start(parts[:, k, :], kparts[:, k % 2, :]).then_inc(ks_stored[k], 16)
                    with sp.Fori(0, B) as b:
                        for p in range(HP):
                            n = b * HP + p
                            sp.wait_ge(k_made, n + 1)
                            sp.wait_ge(nq_made, n + 1)
                            sp.sem_inc(turn_b, 1)
                            sp.dma_start(scratch_qk[bass.ds(n, 1), :, :].rearrange("o p c -> (o p) c"),
                                         qk[p % 2][:, :, :].rearrange("p k l -> p (k l)")).then_inc(qk_stored[p % 2], 16)
                    for c in range(NV):
                        sp.wait_ge(v_made, 2 * c + 2)
                        sp.dma_start(scratch_v[c * VCH:(c + 1) * VCH, :], vs[c % 2][:, :]).then_inc(v_stored[c % 2], 16)
                    for k in range(2):
                        sp.wait_ge(qk_stored[k], 8 * B * HP + 16)
                        sp.wait_ge(v_stored[k], 8 * NV)
                    for k in range(3):
                        sp.wait_ge(ks_stored[k], 16)

                @block.tensor
                def _(pe):
                    pe.wait_ge(weights, 16 * 6)
                    pe.wait_ge(twice_ready, 1)
                    for g in range(NC // 4):
                        if g >= 2:
                            pe.wait_ge((xt_act, xt_vec)[g % 2], g // 2)
                        for k in range(4):
                            tr = pe.transpose(pt[g % 2][:, k * CH:(k + 1) * CH],
                                              twice[:, 4 * g + k, :, :].rearrange("p a d -> p (a d)"), ident[0:CH, 0:CH])
                        tr.then_inc(turned, 1)
                    pe.wait_ge(xt_act, NC // 8)
                    pe.wait_ge(xt_vec, NC // 8)
                    for k in range(2 * B):
                        if k >= 2:
                            pe.wait_ge(ks_kept, k - 1)
                        pe.matmul(pt[k % 2][0:NH, 0:HALF], wkt[:, :], xt[0:D, k * HALF:(k + 1) * HALF],
                                  start=True, stop=True).then_inc(ks_sum, 1)
                    with pe.Fori(0, B // 2) as g:
                        for r in range(2):
                            pe.wait_ge(xb_made, g * 2 + (r + 1))
                            for p in range(HP):
                                n = g * (2 * HP) + (r * HP + p)
                                pe.wait_ge(q_made, n + QCRED - 1)
                                for h in range(2):
                                    mm = pe.matmul(pq[p % 2][:, h, 0:HALF], wq[:, p * 128:(p + 1) * 128],
                                                   xb[r][:, h * HALF:(h + 1) * HALF], start=True, stop=True)
                                mm.then_inc(q_sum, 1)
                    for c in range(NV):
                        for h in range(2):
                            if c:
                                pe.wait_ge(v_made, 2 * c - 1 + h)
                            pe.matmul(pv[h][0:VCH, :], xt[0:D, c * VCH:(c + 1) * VCH], wv[:, h * 512:(h + 1) * 512],
                                      start=True, stop=True).then_inc(v_sum, 1)

                @block.gpsimd
                def _(pool):
                    pool.wait_ge(weights, 16 * 6)
                    pool.wait_ge(xt_act, NC // 8)
                    pool.wait_ge(xt_vec, NC // 8)
                    with pool.Fori(0, B // 2) as g:
                        for r in range(2):
                            pool.wait_ge(q_made, g * (2 * HP) + (r * HP + QCRED - HP))
                            pool.tensor_copy(xb[r][:, :], xt[0:D, bass.ds(g * (2 * L) + r * L, L)]).then_inc(xb_made, 1)

                @block.scalar
                def _(act):
                    act.sem_inc(q_made, QCRED)
                    act.sem_inc(qk_stored[0], 16)
                    act.sem_inc(qk_stored[1], 16)
                    act.wait_ge(var_ready, 1)
                    act.activation(var[:, :], var[:, :], ACT.Sqrt).then_inc(std_ready, 1)
                    act.wait_ge(norm_ready, 1)
                    act.copy(twice[:, :, 1, :], twice[:, :, 0, :]).then_inc(twice_ready, 1)
                    for g in range(0, NC // 4, 2):
                        act.wait_ge(turned, g + 1)
                        act.copy(xt[:, 4 * CH * g:4 * CH * (g + 1)], pt[0][:, 0:4 * CH]).then_inc(xt_act, 1)
                    act.wait_ge(ks_kept, 2 * B)
                    act.copy(kparts[:, 0, :], ks32[:, :]).then_inc(part_act, 1)
                    act.wait_ge(part_vec, 1)
                    act.copy(kparts[:, 1, :], ks32[:, :]).then_inc(part_act, 1)
                    act.wait_ge(part_vec, 2)
                    act.wait_ge(ks_stored[0], 16)
                    act.copy(kparts[:, 0, :], ks32[:, :]).then_inc(part_act, 1)
                    with act.Fori(0, B) as b:
                        for p in range(HP):
                            act.wait_ge(q_made, b * HP + (p + 1 + QCRED))
                            act.mul(qk[p % 2][:, 2, :], qk[p % 2][:, 1, :], -0.5).then_inc(nq_made, 1)

                @block.vector
                def _(vec):
                    links = [0]

                    def link(ins):
                        links[0] += 1
                        ins.then_inc(chain, 1)
                        vec.wait_ge(chain, links[0])

                    layernorm(nc, vec, link, h1[:, :, :], mean, var, cen[:, :, :], twice[:, :, 1, :], var_ready, std_ready, 1)
                    link(vec.tensor_tensor(twice[:, :, 0, :], cen[:, :, :],
                                           var[:, :].unsqueeze(2).to_broadcast([CH, NC, D]), ALU.mult))
                    vec.tensor_tensor(hx[:, :, :], h1[:, :, :], twice[:, :, 0, :], ALU.add).then_inc(norm_ready, 1)
                    for g in range(1, NC // 4, 2):
                        vec.wait_ge(turned, g + 1)
                        vec.tensor_copy(xt[:, 4 * CH * g:4 * CH * (g + 1)], pt[1][:, 0:4 * CH]).then_inc(xt_vec, 1)
                    for k in range(2 * B):
                        vec.wait_ge(ks_sum, k + 1)
                        vec.tensor_copy(ks32[:, k * HALF:(k + 1) * HALF], pt[k % 2][0:NH, 0:HALF]).then_inc(ks_kept, 1)
                    vec.wait_ge(part_act, 1)
                    vec.tensor_tensor(ks32[:, :], ks32[:, :], kparts[:, 0, :], ALU.subtract).then_inc(part_vec, 1)
                    vec.wait_ge(part_act, 2)
                    vec.tensor_tensor(ks32[:, :], ks32[:, :], kparts[:, 1, :], ALU.subtract).then_inc(part_vec, 1)
                    vec.wait_ge(weights, 16 * 6)
                    with vec.Fori(0, B) as b:
                        for p in range(HP):
                            n = b * HP + p
                            vec.wait_ge(qk_stored[p % 2], b * (8 * HP) + (p // 2 + 1) * 16)
                            vec.tensor_scalar(qk[p % 2][:, 0, :], xt[:, bass.ds(b * L, L)], wkc[:, p:p + 1], None,
                                              ALU.mult).then_inc(k_made, 1)
                            vec.wait_ge(q_sum, n + 1)
                            vec.tensor_scalar(qk[p % 2][:, 1, :].rearrange("p (h c) -> p h c", h=2),
                                              pq[p % 2][:, :, 0:HALF], bq[:, p:p + 1], None,
                                              ALU.add).then_inc(q_made, 1)
                    for c in range(NV):
                        if c >= 2:
                            vec.wait_ge(v_stored[c % 2], 16 * (c // 2))
                        for h in range(2):
                            vec.wait_ge(v_sum, 2 * c + h + 1)
                            vec.tensor_tensor(vs[c % 2][:, h * 512:(h + 1) * 512], pv[h][0:VCH, :],
                                              bv[0:VCH, h * 512:(h + 1) * 512], ALU.add).then_inc(v_made, 1)


def phase_attend(nc, sbuf, psum, semaphore, of_acc, ob_acc, ident, window, select, vinit,
                 scratch_qk, scratch_ks, scratch_v):
    with ExitStack() as ctx:
        ring = sbuf(ctx, "ring", [128, RING, QUADS, L])
        qk = [sbuf(ctx, f"qk{k}", [128, 3, L]) for k in range(2)]
        ksum = [sbuf(ctx, f"ksum{k}", [6, L], BF16) for k in range(2)]
        vb = [sbuf(ctx, f"vb{k}", [CH, BC, 2, D]) for k in range(2)]
        vbs = sbuf(ctx, "vbs", [CH, BC, 2, D])
        ex = [sbuf(ctx, f"ex{k}", [128, L]) for k in range(2)]
        ext = sbuf(ctx, "ext", [CH, BC, 2, L + 2])
        vf = [sbuf(ctx, f"vf{k}", [128, 2, VC]) for k in range(3)]
        zero = sbuf(ctx, "zero", [6, 512], BF16)
        rz = sbuf(ctx, "rz", [CH, BC, 2])
        part = sbuf(ctx, "part", [CH, BC, 2, D])
        sc = [psum(ctx, f"sc{k}", [128, 2, 512]) for k in range(2)]
        pv = psum(ctx, "pvf", [128, 2, 512])
        ob = psum(ctx, "ob", [128, 512])
        tr = psum(ctx, "tr", [128, 512])

        vset = semaphore(ctx, "vset")
        turn_c = semaphore(ctx, "turn_c")
        qk_in = [semaphore(ctx, f"qk_in{k}") for k in range(2)]
        vf_in = [semaphore(ctx, f"vf_in{k}") for k in range(3)]
        vf_used = semaphore(ctx, "vf_used")
        made_vec = semaphore(ctx, "made_vec")
        made_act = semaphore(ctx, "made_act")
        ring_free = semaphore(ctx, "ring_free")
        ex_made = semaphore(ctx, "ex_made")
        tr_made = semaphore(ctx, "tr_made")
        tr_kept = semaphore(ctx, "tr_kept")
        pv_free = semaphore(ctx, "pv_free")
        vbs_made = semaphore(ctx, "vbs_made")
        ob_made = semaphore(ctx, "ob_made")
        ob_free = semaphore(ctx, "ob_free")
        chain = semaphore(ctx, "chain_c")
        LINKS = 4

        def pairs(eng, body):
            with eng.Fori(0, B) as b:
                with eng.Fori(0, HP // 2) as g:
                    for par in range(2):
                        body(b * HP + g * 2 + par, b, g * 2 + par, par, b * (HP // 2) + g, b + (1 if par else g))

        def tiles(eng, n, body):
            body(n * NT + 1, 0, 0, n * STEPS, 0, "first")
            with eng.Fori(0, (FULL - 1) // 2) as u:
                for r in range(2):
                    t = u * 2 + (1 + r)
                    body(n * NT + t + 1, t, t * TILE, n * STEPS + t * ROWS, 1 - r, "inner")
            body(n * NT + FULL + 1, FULL, FULL * TILE, n * STEPS + FULL * ROWS, FULL % 2, "last")

        def members(kind):
            rows, count = (LROWS, LASTN) if kind == "last" else (ROWS, TILE)
            return [[(j, rows * j + i) for j in range(QUADS) if rows * j + i < count] for i in range(rows)]

        with nc.Block() as block:
            @block.sync
            def _(sp):
                sp.wait_ge(vset, 2)

                def tile(T, t, s0, G, par, kind, b, hp):
                    k = 2 if kind == "last" else par
                    sp.wait_ge(vf_used, T + 1)
                    sp.sem_inc(turn_c, 1)
                    rows = LROWS if kind == "last" else TILE
                    for j in range(QUADS if kind == "last" else 1):
                        cnt = min(rows, LASTN - rows * j) if kind == "last" else TILE
                        for h in range(2):
                            p0 = 32 * j + h
                            sp.dma_start(vf[k][p0:p0 + 2 * cnt - 1:2, h, 0:D],
                                         scratch_v[bass.ds(b * L + s0 + rows * j, cnt),
                                                   bass.ds(hp * 2 * D + h * D, D)]).then_inc(vf_in[k], 16)

                pairs(sp, lambda n, b, hp, par, m, back: tiles(sp, n, lambda *a: tile(*a, b, hp)))

            @block.gpsimd
            def _(pool):
                def load(n, b, hp, par, m, back):
                    pool.wait_ge(ob_made, n + 2)
                    pool.dma_start(qk[par][:, :, :].rearrange("p k l -> p (k l)"),
                                   scratch_qk[bass.ds(n, 1), :, :].rearrange("o p c -> (o p) c")).then_inc(qk_in[par], 16)
                    pool.dma_start(ksum[par][:, :],
                                   scratch_ks[bass.ds(hp * 6, 6), bass.ds(b * L, L)]).then_inc(qk_in[par], 16)
                    pool.dma_start(vb[par][:, :, :, :].rearrange("p c k d -> p c (k d)"),
                                   scratch_v[bass.ds(b * L, L), bass.ds(hp * 2 * D + NH * D, 2 * D)]
                                   .rearrange("(c p) d -> p c d", p=CH)).then_inc(qk_in[par], 16)

                pairs(pool, load)

            @block.tensor
            def _(pe):
                pe.wait_ge(vset, 2)

                def after(T, par, k, loads):
                    pe.wait_ge(ex_made, T + 1)
                    pe.wait_ge(vf_in[k], loads)
                    for c in range(BC):
                        mm = pe.matmul(pv[0:CH, c // 3, (c % 3) * 2 * VC:(c % 3 + 1) * 2 * VC],
                                       ex[par][:, c * CH:(c + 1) * CH],
                                       vf[k][:, :, :].rearrange("p k v -> p (k v)"),
                                       start=False, stop=(k == 2), skip_group_check=True)
                    mm.then_inc(vf_used, 1)

                def turn(T, par, r):
                    pe.wait_ge(tr_kept, T * 2 + r + 1)
                    for c in range(3):
                        x = pe.transpose(tr[0:CH, c * 128:(c + 1) * 128],
                                         ex[par][:, (3 * r + c) * CH:(3 * r + c + 1) * CH], ident[:, :])
                    x.then_inc(tr_made, 1)

                def backward(c, n):
                    if c == 0:
                        pe.wait_ge(vbs_made, n + 1)
                        pe.wait_ge(tr_kept, n * NT * 2 + 3)
                        pe.wait_ge(ob_free, n + 1)
                    for k in range(2):
                        for h in range(2):
                            mm = pe.matmul(ob[64 * h:64 * h + 64, 0:HALF], vbs[:, c, k, :],
                                           ext[:, c, k, h * HALF:(h + 1) * HALF],
                                           start=(c + k == 0), stop=(c == BC - 1 and k == 1))
                    if c == BC - 1:
                        mm.then_inc(ob_made, 1)

                def tile(T, G, par, kind, npar, before, behind):
                    bank = sc[par]
                    for h in range(2):
                        pe.matmul(bank[:, h, 0:HALF], select[:, int(kind == "last"), :],
                                  ksum[npar][:, h * HALF:(h + 1) * HALF],
                                  start=True, stop=False, skip_group_check=True)
                    steps = members(kind)
                    for i, js in enumerate(steps):
                        pe.wait_ge(made_vec, G + i + 1)
                        pe.wait_ge(made_act, G + i + 1)
                        for h in range(2):
                            for j, s in js:
                                mm = pe.matmul(bank[32 * j:32 * j + 32, h, 0:HALF], window[:, 30 - 2 * i:62 - 2 * i],
                                               ring[:, i % RING, j, h * HALF:(h + 1) * HALF],
                                               start=False, stop=(i == len(steps) - 1 or (j, s + 1) == (QUADS - 1, LASTN)),
                                               skip_group_check=True)
                        mm.then_inc(ring_free, 1)
                        if i == 4:
                            after(*before)
                        if i in (5, 8):
                            turn(before[0], before[1], i // 8)
                        if behind is not None and i >= ROWS - BC:
                            backward(i - (ROWS - BC), behind)

                def open_sums():
                    for g in range(2):
                        pe.matmul(pv[0:CH, g, 0:3 * 2 * VC], zero[:, 0:CH], zero[:, 0:3 * 2 * VC],
                                  start=True, stop=False, skip_group_check=True)

                def pair(n, b, hp, npar, m, back):
                    pe.wait_ge(qk_in[npar], (m + 1) * 48)
                    tile(n * NT + 1, n * STEPS, 0, "first", npar,
                         (n * NT, FULL % 2, 2, n * 16 * 2 * QUADS + 16), n)
                    pe.wait_ge(pv_free, n + 1)
                    open_sums()
                    with pe.Fori(0, (FULL - 1) // 2) as u:
                        for r in range(2):
                            T = n * NT + (u * 2 + (2 + r))
                            tile(T, n * STEPS + u * (2 * ROWS) + (1 + r) * ROWS, 1 - r, "inner", npar,
                                 (T - 1, r, r, (n * (6 - r) + u + 1) * 32), None)
                    T = n * NT + FULL + 1
                    tile(T, n * STEPS + FULL * ROWS, FULL % 2, "last", npar, (T - 1, 0, 0, (n * 6 + 6) * 32), None)

                open_sums()
                for h in range(2):
                    mm = pe.matmul(sc[FULL % 2][:, h, 0:HALF], zero[:, 0:128], zero[:, 0:HALF], start=True, stop=True)
                mm.then_inc(ring_free, RING)
                pairs(pe, pair)
                N = B * HP
                after(N * NT, FULL % 2, 2, N * 16 * 2 * QUADS + 16)
                for r in range(2):
                    turn(N * NT, FULL % 2, r)
                for c in range(BC):
                    backward(c, N)

            def keep_half(copy, r, s0, kind):
                src = tr[0:CH, 0:384].rearrange("p (c m k) -> p c m k", c=3, k=2)
                if kind == "last":
                    for k in range(2):
                        for c in range(3):
                            dst = ext[:, 3 * r + c, k, FULL * TILE:FULL * TILE + QUADS * LROWS]
                            x = copy(dst.rearrange("p (j i) -> p j i", j=QUADS),
                                     src[:, c, :, k].rearrange("p (j i) -> p j i", j=QUADS)[:, :, 0:LROWS])
                    return x
                for k in range(2):
                    x = copy(ext[:, 3 * r:3 * r + 3, k, bass.ds(s0, TILE)], src[:, :, :, k])
                return x

            @block.scalar
            def _(act):
                act.sem_inc(ob_made, 2)
                act.sem_inc(vf_used, 2)
                act.sem_inc(vf_in[2], 16)
                act.sem_inc(tr_kept, 1)
                act.sem_inc(ob_free, 1)

                def finish(par):
                    act.activation(ex[par][:, :].rearrange("p (h c) -> p h c", h=2), sc[par][:, :, 0:HALF],
                                   ACT.Exp, scale=-2.0 / D ** 0.5).then_inc(ex_made, 1)

                def keep(T, s0, kind):
                    act.wait_ge(tr_made, T * 2 + 2)
                    keep_half(act.copy, 1, s0, kind).then_inc(tr_kept, 1)

                def tile(T, s0, G, par, kind, npar, before):
                    rows = members(kind)
                    for i, js in enumerate(rows):
                        act.wait_ge(ring_free, G + i + 1)
                        for j, s in js:
                            if on_scalar(i, j):
                                x = act.activation(ring[:, i % RING, j, :], qk[npar][:, 0, :], ACT.Abs,
                                                   bias=qk[npar][:, 2, bass.ds(s0 + s, 1)], scale=0.5)
                        x.then_inc(made_act, 1)
                        if i == RING - 1:
                            finish(1 - par)
                        if i == min(12, len(rows) - 1):
                            keep(*before)

                def pair(n, b, hp, npar, m, back):
                    act.wait_ge(qk_in[npar], (m + 1) * 48)
                    tile(n * NT + 1, 0, n * STEPS, 0, "first", npar, (n * NT, FULL * TILE, "last"))
                    with act.Fori(0, (FULL - 1) // 2) as u:
                        for r in range(2):
                            t = u * 2 + (1 + r)
                            T = n * NT + t + 1
                            tile(T, t * TILE, n * STEPS + t * ROWS, 1 - r, "inner", npar,
                                 (T - 1, (t - 1) * TILE, "inner"))
                    T = n * NT + FULL + 1
                    tile(T, FULL * TILE, n * STEPS + FULL * ROWS, FULL % 2, "last", npar,
                         (T - 1, (FULL - 1) * TILE, "inner"))

                pairs(act, pair)
                N = B * HP
                act.wait_ge(ring_free, N * STEPS + RING)
                finish(FULL % 2)
                keep(N * NT, FULL * TILE, "last")

            @block.vector
            def _(vec):
                vec.memset(zero[:, :], 0.0)
                vec.memset(vb[1][:, :, :, :], 0.0)
                vec.memset(ext[:, :, :, :], 0.0)
                for k in range(3):
                    x = vec.memset(vf[k][:, :, :], 0.0)
                x.then_inc(vset, 1)
                vec.wait_ge(vset, 1)
                for k in range(3):
                    x = vec.tensor_copy(vf[k][:, :, D:VC].rearrange("p h o -> p (h o)"),
                                        vinit[:, 2 * (k // 2):2 * (k // 2) + 2])
                x.then_inc(vset, 1)

                def keep(T, s0, kind):
                    vec.wait_ge(tr_made, T * 2 + 1)
                    keep_half(vec.tensor_copy, 0, s0, kind).then_inc(tr_kept, 1)

                def link(ins, level):
                    ins.then_inc(chain, 1)
                    vec.wait_ge(chain, level)

                def weigh(n, npar):
                    vec.wait_ge(vf_used, n * NT + 3)
                    for g in range(2):
                        sums = pv[0:CH, g, 0:3 * 2 * VC].rearrange("p (c k v) -> p c k v", c=3, k=2)
                        x = vec.tensor_scalar(rz[:, 3 * g:3 * g + 3, :].unsqueeze(3), sums[:, :, :, D:VC], 1.0, None, ALU.add)
                    link(x, n * LINKS + 1)
                    link(vec.reciprocal(rz[:, :, :], rz[:, :, :]), n * LINKS + 2)
                    vec.tensor_tensor(vbs[:, :, :, :].rearrange("p c k d -> p (c k) d"),
                                      vb[npar][:, :, :, :].rearrange("p c k d -> p (c k) d"),
                                      rz[:, :, :].rearrange("p c k -> p (c k)").unsqueeze(2)
                                      .to_broadcast([CH, 2 * BC, D]), ALU.mult).then_inc(vbs_made, 1)

                def forward(n, back):
                    for g in range(2):
                        for k in range(2):
                            sums = pv[0:CH, g, 0:3 * 2 * VC].rearrange("p (c k v) -> p c k v", c=3, k=2)
                            x = vec.tensor_tensor(part[:, 3 * g:3 * g + 3, k, :], sums[:, :, k, 0:D],
                                                  rz[:, 3 * g:3 * g + 3, k].unsqueeze(2).to_broadcast([CH, 3, D]), ALU.mult)
                    x.then_inc(pv_free, 1)
                    vec.wait_ge(pv_free, n + 1)
                    mine = of_acc[:, bass.ds(back * BC, BC), :]
                    link(vec.tensor_tensor(mine, mine, part[:, :, 0, :], ALU.add), n * LINKS + 3)
                    link(vec.tensor_tensor(mine, mine, part[:, :, 1, :], ALU.add), n * LINKS + 4)

                def backward(n, back):
                    vec.wait_ge(ob_made, n + 3)
                    vec.wait_ge(ob_free, n + 1)
                    mine = ob_acc[:, bass.ds(back, 1), :].rearrange("p o c -> p (o c)")
                    vec.tensor_tensor(mine, mine, ob[:, 0:HALF], ALU.add).then_inc(ob_free, 1)

                def tile(s0, G, kind, npar, before, behind):
                    for i, js in enumerate(members(kind)):
                        vec.wait_ge(ring_free, G + i + 1)
                        for j, s in js:
                            if not on_scalar(i, j):
                                x = vec.tensor_scalar(ring[:, i % RING, j, :], qk[npar][:, 0, :],
                                                      qk[npar][:, 1, bass.ds(s0 + s, 1)],
                                                      qk[npar][:, 2, bass.ds(s0 + s, 1)], ALU.max, ALU.add)
                        x.then_inc(made_vec, 1)
                        if i == 9:
                            keep(*before)
                            if behind:
                                weigh(behind[0], 1 - npar)
                        if behind and i == 11:
                            forward(*behind)

                def pair(n, b, hp, npar, m, back):
                    vec.wait_ge(qk_in[npar], (m + 1) * 48)
                    tile(0, n * STEPS, "first", npar, (n * NT, FULL * TILE, "last"), (n, back))
                    with vec.Fori(0, (FULL - 1) // 2) as u:
                        for r in range(2):
                            t = u * 2 + (1 + r)
                            tile(t * TILE, n * STEPS + t * ROWS, "inner", npar,
                                 (n * NT + t, (t - 1) * TILE, "inner"), None)
                    tile(FULL * TILE, n * STEPS + FULL * ROWS, "last", npar,
                         (n * NT + FULL, (FULL - 1) * TILE, "inner"), None)
                    backward(n, back)

                pairs(vec, pair)
                N = B * HP
                keep(N * NT, FULL * TILE, "last")
                weigh(N, (N - 1) % 2)
                forward(N, B)
                backward(N, B)


def phase_feed(nc, A, out, sbuf, psum, semaphore, hx, of_acc, ob_acc, ident):
    with ExitStack() as ctx:
        x2t = sbuf(ctx, "x2t", [128, TOK])
        h2 = sbuf(ctx, "h2", [CH, NC, D])
        wgt = sbuf(ctx, "wgt", [D, NE])
        bg = sbuf(ctx, "bg", [CH, NE])
        tri = sbuf(ctx, "tri", [CH, NE, NE])
        w1t = sbuf(ctx, "w1t", [128, NE, 128])
        b1c = sbuf(ctx, "b1c", [128, 2 * NE])
        w2t = sbuf(ctx, "w2t", [128, NE, 2, D])
        b2 = sbuf(ctx, "b2", [CH, NE, D])
        comb = sbuf(ctx, "comb", [CH, NC, NE])
        weights = semaphore(ctx, "weights_d")
        NW = 9
        with ExitStack() as inner:
            o = sbuf(inner, "o", [CH, NC, D])
            sg = sbuf(inner, "sg", [CH, NC, D])
            cen = sbuf(inner, "cen_d", [CH, NC, D])
            twice = sbuf(inner, "twice_d", [CH, NC, 2, D])
            gt = sbuf(inner, "gt", [D, TOK])
            fant = sbuf(inner, "fant", [D, D])
            fb = sbuf(inner, "fb", [CH, D])
            mean = sbuf(inner, "mean_d", [CH, NC])
            var = sbuf(inner, "var_d", [CH, NC])
            gs = sbuf(inner, "gs", [CH, NC, NE])
            gmax = sbuf(inner, "gmax", [CH, NC])
            gsum = sbuf(inner, "gsum", [CH, NC])
            gex = sbuf(inner, "gex", [CH, NC, NE])
            rank = sbuf(inner, "rank", [CH, NC, NE])
            big = sbuf(inner, "big", [CH, NC // 2, NE, NE])
            eqs = sbuf(inner, "eqs", [CH, NC // 2, NE, NE])
            pa = [psum(inner, f"pa{k}", [128, 512]) for k in range(7)]
            pg = psum(inner, "pg", [128, 512])
            chain = semaphore(inner, "chain_d")
            back_t = semaphore(inner, "back_t")
            o_made = semaphore(inner, "o_made")
            sg_made = semaphore(inner, "sg_made")
            g_made = semaphore(inner, "g_made")
            g_turned = semaphore(inner, "g_turned")
            gt_act = semaphore(inner, "gt_act")
            gt_vec = semaphore(inner, "gt_vec")
            y_sum = semaphore(inner, "y_sum")
            var_ready = semaphore(inner, "var_ready_d")
            std_ready = semaphore(inner, "std_ready_d")
            norm_ready = semaphore(inner, "norm_ready_d")
            twice_ready = semaphore(inner, "twice_ready_d")
            turned = semaphore(inner, "turned_d")
            xt_act = semaphore(inner, "xt_act_d")
            xt_vec = semaphore(inner, "xt_vec_d")
            gate_sum = semaphore(inner, "gate_sum")
            shifted = semaphore(inner, "shifted")
            gexp = semaphore(inner, "gexp")
            with nc.Block() as block:
                @block.sync
                def _(sp):
                    sp.dma_start(fant[:, :], A["fant"]).then_inc(weights, 16)
                    sp.dma_start(fb[:, :], A["fb"].partition_broadcast(CH)).then_inc(weights, 16)
                    sp.dma_start(wgt[:, :], A["wgt"]).then_inc(weights, 16)
                    sp.dma_start(bg[:, :], A["bg"].partition_broadcast(CH)).then_inc(weights, 16)
                    sp.dma_start(tri[:, :, :].rearrange("p a b -> p (a b)"),
                                 A["tri"].partition_broadcast(CH)).then_inc(weights, 16)
                    sp.dma_start(w1t[:, :, :].rearrange("p e m -> p (e m)"), A["w1t"]).then_inc(weights, 16)
                    sp.dma_start(b1c[:, :], A["b1c"]).then_inc(weights, 16)
                    sp.dma_start(w2t[:, :, :, :].rearrange("p e h d -> p (e h d)"), A["w2t"]).then_inc(weights, 16)
                    sp.dma_start(b2[:, :, :].rearrange("p e d -> p (e d)"),
                                 A["b2"].partition_broadcast(CH)).then_inc(weights, 16)
                    sp.wait_ge(weights, 16 * NW)

                @block.tensor
                def _(pe):
                    for g in range(B):
                        h = g // (B // 2)
                        for k in range(2 * 3):
                            b, q = 2 * (g % (B // 2)) + k // 3, k % 3
                            mm = pe.transpose((pa + [pg])[g][0:CH, D * k:D * k + D],
                                              ob_acc[64 * h:64 * h + 64, 1 + b, q * CH:(q + 1) * CH],
                                              ident[64 * h:64 * h + 64, 64 * h:64 * h + 64])
                        mm.then_inc(back_t, 1)
                    pe.wait_ge(g_made, 1)
                    for g in range(NC // 4):
                        if g >= 2:
                            pe.wait_ge((gt_act, gt_vec)[g % 2], g // 2)
                        for k in range(4):
                            mm = pe.transpose(pa[g % 2][0:D, k * CH:(k + 1) * CH], sg[:, 4 * g + k, :], ident[0:CH, 0:CH])
                        mm.then_inc(g_turned, 1)
                    pe.wait_ge(weights, 16 * NW)
                    pe.wait_ge(gt_act, NC // 8)
                    pe.wait_ge(gt_vec, NC // 8)
                    for g in range(NC // 8):
                        for k in range(8):
                            c = 8 * g + k
                            mm = pe.matmul(pa[g][0:CH, D * k:D * k + D], gt[:, c * CH:(c + 1) * CH], fant[:, :],
                                           start=True, stop=True)
                        mm.then_inc(y_sum, 1)
                    pe.wait_ge(twice_ready, 1)
                    for g in range(NC // 4):
                        if g >= 2:
                            pe.wait_ge((xt_act, xt_vec)[g % 2], g // 2)
                        for k in range(4):
                            mm = pe.transpose(pa[g % 2][:, k * CH:(k + 1) * CH],
                                              twice[:, 4 * g + k, :, :].rearrange("p a d -> p (a d)"), ident[0:CH, 0:CH])
                        mm.then_inc(turned, 1)
                    pe.wait_ge(xt_act, NC // 8)
                    pe.wait_ge(xt_vec, NC // 8)
                    for c in range(NC):
                        mm = pe.matmul(pg[0:CH, NE * c:NE * c + NE], x2t[0:D, c * CH:(c + 1) * CH], wgt[:, :],
                                       start=True, stop=True)
                    mm.then_inc(gate_sum, 1)

                @block.scalar
                def _(act):
                    act.wait_ge(o_made, 1)
                    act.activation(sg[:, :, :], o[:, :, :], ACT.Sigmoid, scale=1.702).then_inc(sg_made, 1)
                    for g in range(0, NC // 4, 2):
                        act.wait_ge(g_turned, g + 1)
                        act.copy(gt[:, 4 * CH * g:4 * CH * (g + 1)], pa[0][0:D, 0:4 * CH]).then_inc(gt_act, 1)
                    act.wait_ge(var_ready, 1)
                    act.activation(var[:, :], var[:, :], ACT.Sqrt).then_inc(std_ready, 1)
                    act.wait_ge(norm_ready, 1)
                    act.copy(twice[:, :, 1, :], twice[:, :, 0, :]).then_inc(twice_ready, 1)
                    for g in range(0, NC // 4, 2):
                        act.wait_ge(turned, g + 1)
                        act.copy(x2t[:, 4 * CH * g:4 * CH * (g + 1)], pa[0][:, 0:4 * CH]).then_inc(xt_act, 1)
                    act.wait_ge(shifted, 1)
                    act.activation(gex[:, :, :], gex[:, :, :], ACT.Exp).then_inc(gexp, 1)

                @block.vector
                def _(vec):
                    links = [0]

                    def link(ins):
                        links[0] += 1
                        ins.then_inc(chain, 1)
                        vec.wait_ge(chain, links[0])

                    halves = [buf.rearrange("p (b h q) d -> p b h q d", b=B, h=2) for buf in (o[:, :, :], of_acc[:, BC:, :])]
                    for g in range(B):
                        vec.wait_ge(back_t, g + 1)
                        h, b = g // (B // 2), 2 * (g % (B // 2))
                        x = vec.tensor_tensor(halves[0][:, b:b + 2, h, :, :], halves[1][:, b:b + 2, h, :, :],
                                              (pa + [pg])[g][0:CH, 0:6 * D].rearrange("p (b q d) -> p b q d", b=2, q=3),
                                              ALU.add)
                    x.then_inc(o_made, 1)
                    vec.wait_ge(sg_made, 1)
                    vec.wait_ge(o_made, 1)
                    vec.tensor_tensor(sg[:, :, :], o[:, :, :], sg[:, :, :], ALU.mult).then_inc(g_made, 1)
                    for g in range(1, NC // 4, 2):
                        vec.wait_ge(g_turned, g + 1)
                        vec.tensor_copy(gt[:, 4 * CH * g:4 * CH * (g + 1)], pa[1][0:D, 0:4 * CH]).then_inc(gt_vec, 1)
                    vec.wait_ge(weights, 16 * NW)
                    link(vec.tensor_tensor(hx[:, :, :], hx[:, :, :],
                                           fb[:, :].unsqueeze(1).to_broadcast([CH, NC, D]), ALU.add))
                    for g in range(NC // 8):
                        vec.wait_ge(y_sum, g + 1)
                        x = vec.tensor_tensor(h2[:, 8 * g:8 * g + 8, :], hx[:, 8 * g:8 * g + 8, :],
                                              pa[g][0:CH, :].rearrange("p (k d) -> p k d", k=8), ALU.add)
                    link(x)
                    layernorm(nc, vec, link, h2[:, :, :], mean, var, cen[:, :, :], o[:, :, :], var_ready, std_ready, 1)
                    vec.tensor_tensor(twice[:, :, 0, :], cen[:, :, :],
                                      var[:, :].unsqueeze(2).to_broadcast([CH, NC, D]), ALU.mult).then_inc(norm_ready, 1)
                    for g in range(1, NC // 4, 2):
                        vec.wait_ge(turned, g + 1)
                        vec.tensor_copy(x2t[:, 4 * CH * g:4 * CH * (g + 1)], pa[1][:, 0:4 * CH]).then_inc(xt_vec, 1)
                    vec.wait_ge(gate_sum, 1)
                    link(vec.tensor_tensor(gs[:, :, :], pg[0:CH, 0:NC * NE].rearrange("p (c e) -> p c e", e=NE),
                                           bg[:, :].unsqueeze(1).to_broadcast([CH, NC, NE]), ALU.add))
                    link(vec.reduce_max(gmax[:, :], gs[:, :, :], axis=AX.X))
                    vec.tensor_tensor(gex[:, :, :], gs[:, :, :], gmax[:, :].unsqueeze(2).to_broadcast([CH, NC, NE]),
                                      ALU.subtract).then_inc(shifted, 1)
                    for half in range(2):
                        cs = slice(half * NC // 2, (half + 1) * NC // 2)
                        n2 = NC // 2
                        for e in range(NE):
                            me = gs[:, cs, e:e + 1].to_broadcast([CH, n2, NE])
                            vec.tensor_tensor(big[:, :, e, :], gs[:, cs, :], me, ALU.is_gt)
                            x = vec.tensor_tensor(eqs[:, :, e, :], gs[:, cs, :], me, ALU.is_equal)
                        link(x)
                        link(vec.tensor_tensor(eqs[:, :, :, :].rearrange("p c a b -> p c (a b)"),
                                               eqs[:, :, :, :].rearrange("p c a b -> p c (a b)"),
                                               tri[:, :, :].rearrange("p a b -> p (a b)").unsqueeze(1)
                                               .to_broadcast([CH, n2, NE * NE]), ALU.mult))
                        link(vec.tensor_tensor(big[:, :, :, :].rearrange("p c a b -> p (c a b)"),
                                               big[:, :, :, :].rearrange("p c a b -> p (c a b)"),
                                               eqs[:, :, :, :].rearrange("p c a b -> p (c a b)"), ALU.add))
                        link(vec.reduce_sum(rank[:, cs, :].rearrange("p c e -> p (c e)"),
                                            big[:, :, :, :].rearrange("p c a b -> p (c a) b"), axis=AX.X))
                    link(vec.tensor_scalar(rank[:, :, :], rank[:, :, :], 1.5, None, ALU.is_lt))
                    vec.wait_ge(gexp, 1)
                    link(vec.tensor_tensor(gex[:, :, :], gex[:, :, :], rank[:, :, :], ALU.mult))
                    link(vec.reduce_sum(gsum[:, :], gex[:, :, :], axis=AX.X))
                    link(vec.reciprocal(gsum[:, :], gsum[:, :]))
                    link(vec.tensor_tensor(comb[:, :, :], gex[:, :, :],
                                           gsum[:, :].unsqueeze(2).to_broadcast([CH, NC, NE]), ALU.mult))

        with ExitStack() as inner:
            xc = [sbuf(inner, f"xc{r}", [128, EC]) for r in range(2)]
            hid = [[sbuf(inner, f"hid{r}_{k}", [128, EC]) for k in range(2 * NE)] for r in range(2)]
            wy = [sbuf(inner, f"wy{k}", [CH, NE, D]) for k in range(2)]
            red = [sbuf(inner, f"red{k}", [CH, D]) for k in range(2)]
            res = [sbuf(inner, f"res{k}", [CH, EC // CH, D]) for k in range(2)]
            pu = [psum(inner, f"pu{k}", [128, 512]) for k in range(4)]
            py = [psum(inner, f"py{k}", [128, 512]) for k in range(4)]
            xc_made = semaphore(inner, "xc_made")
            up = semaphore(inner, "up")
            relu_act = semaphore(inner, "relu_act")
            down = semaphore(inner, "down")
            y_free = semaphore(inner, "y_free")
            chain = semaphore(inner, "chain_e")
            res_made = semaphore(inner, "res_made")
            turn_e = semaphore(inner, "turn_e")
            res_out = [semaphore(inner, f"res_out{k}") for k in range(2)]
            NQ = TOK // EC
            SUB = EC // CH
            view = out.rearrange("b t d -> (b t) d")
            LK = 2 * SUB
            with nc.Block() as block:
                @block.sync
                def _(sp):
                    with sp.Fori(0, NQ // 2) as it:
                        for r in range(2):
                            q = it * 2 + r
                            sp.wait_ge(res_made, q + 1)
                            sp.sem_inc(turn_e, 1)
                            sp.dma_start(view[bass.ds(q * EC, EC), :].rearrange("(c p) d -> p c d", p=CH),
                                         res[r][:, :, :]).then_inc(res_out[r], 16)
                    for r in range(2):
                        sp.wait_ge(res_out[r], 8 * NQ + 16)

                @block.gpsimd
                def _(pool):
                    with pool.Fori(0, NQ // 2) as it:
                        for r in range(2):
                            q = it * 2 + r
                            pool.wait_ge(up, q * (2 * NE) + 2 * NE)
                            pool.tensor_copy(xc[r][:, :], x2t[:, bass.ds(q * EC, EC)]).then_inc(xc_made, 1)

                @block.tensor
                def _(pe):
                    def ups(q, r):
                        pe.wait_ge(xc_made, q + 1)
                        for e in range(NE):
                            pe.wait_ge(relu_act, q * (2 * NE) + (2 * e + 2))
                            for h in range(2):
                                pe.matmul(pu[(2 * e + h) % 4][:, 0:EC], w1t[64 * h:64 * h + 64, e, :],
                                          xc[r][64 * h:64 * h + 64, :],
                                          start=True, stop=True).then_inc(up, 1)

                    def downs(q, r):
                        pe.wait_ge(relu_act, q * (2 * NE) + (2 * NE + 4))
                        for s in range(SUB):
                            pe.wait_ge(y_free, q * SUB + (s + 1))
                            for e in range(NE):
                                for h in range(2):
                                    mm = pe.matmul(py[s][0:CH, e * D:(e + 1) * D],
                                                   hid[r][2 * e + h][:, s * CH:(s + 1) * CH], w2t[:, e, h, :],
                                                   start=(h == 0), stop=(h == 1))
                            mm.then_inc(down, 1)

                    with pe.Fori(0, NQ // 2) as it:
                        for r in range(2):
                            ups(it * 2 + r, r)
                            downs(it * 2 + r, r)

                @block.scalar
                def _(act):
                    act.sem_inc(up, 4 * NE)
                    act.sem_inc(relu_act, 4)
                    act.sem_inc(y_free, 4)
                    act.sem_inc(res_out[0], 16)
                    act.sem_inc(res_out[1], 16)
                    with act.Fori(0, NQ // 2) as it:
                        for r in range(2):
                            q = it * 2 + r
                            act.wait_ge(y_free, q * SUB + 1)
                            for k in range(2 * NE):
                                act.wait_ge(up, q * (2 * NE) + (k + 1 + 4 * NE))
                                act.activation(hid[r][k][:, :], pu[k % 4][:, 0:EC], ACT.Relu,
                                               bias=b1c[:, k:k + 1]).then_inc(relu_act, 1)

                @block.vector
                def _(vec):
                    with vec.Fori(0, NQ // 2) as it:
                        for r in range(2):
                            q = it * 2 + r
                            at = [0]

                            def link(ins):
                                at[0] += 1
                                ins.then_inc(chain, 1)
                                vec.wait_ge(chain, q * LK + at[0])

                            vec.wait_ge(res_out[r], it * 16 + 16)
                            for s in range(SUB):
                                vec.wait_ge(down, q * SUB + (s + 1))
                                w = wy[s % 2]
                                x = vec.tensor_tensor(w[:, :, :], py[s][0:CH, :].rearrange("p (e d) -> p e d", e=NE),
                                                      b2[:, :, :], ALU.add)
                                x.then_inc(y_free, 1)
                                vec.wait_ge(y_free, q * SUB + (s + 5))
                                link(vec.tensor_tensor(w[:, :, :], w[:, :, :],
                                                       comb[:, bass.ds(q * SUB + s, 1), :].rearrange("p o e -> p (o e)")
                                                       .unsqueeze(2).to_broadcast([CH, NE, D]), ALU.mult))
                                link(vec.reduce_sum(red[s % 2][:, :], w[:, :, :].rearrange("p e d -> p d e"), axis=AX.X))
                                x = vec.tensor_tensor(res[r][:, s, :], red[s % 2][:, :],
                                                      h2[:, bass.ds(q * SUB + s, 1), :].rearrange("p o d -> p (o d)"), ALU.add)
                                if s == SUB - 1:
                                    x.then_inc(res_made, 1)


def arrange(inputs):
    import numpy as np
    g = {k: np.asarray(v) for k, v in inputs.items()}
    f = np.float32
    xf = g["x"].transpose(1, 0, 2).reshape(DIMS, TOK)
    xr = g["x"][:, :, ::-1].transpose(1, 0, 2).reshape(DIMS, TOK)
    ones = np.ones((3, TOK), f)
    z4, z64 = np.zeros((DIMS, D), f), np.zeros((D, D), f)
    w1, w2, w3, w4 = (g[f"L0_tok_W{k}"].T for k in (1, 2, 3, 4))
    b1, b2, b3, b4 = (g[f"L0_tok_b{k}"][None, :] for k in (1, 2, 3, 4))
    w, bias, wk = g["L0_attn_wqv_w"], g["L0_attn_wqv_b"], g["L0_attn_wk"]
    window = np.zeros((128, 62), f)
    window[0:64, 30] = 1.0
    window[64:128, 31] = 1.0
    select = np.zeros((6, 2, 128), f)
    vinit = np.zeros((128, 2, 2), f)
    for p in range(128):
        j, i, k = p // 32, (p % 32) // 2, p % 2
        for last in range(2):
            if not last or (i < LROWS and LROWS * j + i < LASTN):
                vinit[p, last, k] = 1.0
                if not on_scalar(i, j):
                    select[3 * k:3 * k + 3, last, p] = -0.5
    tri = np.zeros((NE, NE), f)
    for e in range(NE):
        tri[e, :e] = 1.0
    W1, W2 = g["L0_ffn_W1"], g["L0_ffn_W2"]
    return {
        "x10": np.concatenate([xf, xr, ones[0:2]]), "x7": np.concatenate([xf, ones]),
        "w1b": np.concatenate([np.concatenate([w1, z4], 1), np.concatenate([z4, w1], 1),
                               np.concatenate([b1, b1], 1), np.concatenate([b2, b2], 1)]),
        "w2b": np.concatenate([np.concatenate([w2, z64], 1), np.concatenate([z64, w2], 1)]),
        "w4d": np.concatenate([w4, w4]), "w3b": np.concatenate([w3, b3, b4, b4]),
        "ident": np.eye(128, dtype=f), "window": window, "select": select.reshape(6, 256), "vinit": vinit.reshape(128, 4),
        "wq": w[0:NH * D].T, "wv": w[NH * D:].T, "bq": bias[0:NH * D].reshape(HP, 128).T, "bv": bias[NH * D:],
        "wkc": wk.reshape(HP, 128).T, "wkt": wk.T,
        "fant": g["L0_attn_fanin_w"].T, "fb": g["L0_attn_fanin_b"],
        "wgt": g["L0_ffn_Wg"].T, "bg": g["L0_ffn_bg"], "tri": tri.reshape(-1),
        "w1t": W1.reshape(NE, 2, 128, D).transpose(1, 3, 0, 2).reshape(128, NE * 128),
        "b1c": g["L0_ffn_b1"].reshape(2 * NE, 128).T,
        "w2t": W2.reshape(NE, D, 2, 128).transpose(3, 0, 2, 1).reshape(128, NE * 2 * D),
        "b2": g["L0_ffn_b2"].reshape(-1),
    }


def kernel(**inputs):
    import numpy as np
    import concourse.bacc as _bacc
    from concourse.bass_utils import run_bass_kernel_spmd as _run

    nc = _bacc.Bacc("TRN2", target_bir_lowering=False, num_devices=1)
    arrays, aps = {}, {}
    for name, a in arrange(inputs).items():
        a = np.ascontiguousarray(a)
        arrays[f"in_{name}"] = a
        aps[name] = nc.dram_tensor(f"in_{name}", a.shape, F32, kind="ExternalInput").ap()
    out = nc.dram_tensor("out_h", (B, L, D), F32, kind="ExternalOutput").ap()
    build(nc, aps, out)
    r = _run(nc, [arrays], core_ids=[0])
    return r.results[0]["out_h"]
```

```python
import concourse.bass as bass
from concourse import mybir
from contextlib import ExitStack

F32 = mybir.dt.float32
BF16 = mybir.dt.bfloat16
ALU = mybir.AluOpType
ACT = mybir.ActivationFunctionType
AX = mybir.AxisListType

B, DIMS, L, D = 8, 4, 750, 64
TOK = B * L
ROUNDS = 8
HALF = L // 2
CH = 125
NC = TOK // CH
BC = L // CH
NH = 8
HP = NH // 2
NE, HID = 8, 256
EPS = 1e-5
QUADS = 4
ROWS = 16
TILE = QUADS * ROWS
FULL = L // TILE
LASTN = L - FULL * TILE
LROWS = -(-LASTN // QUADS)
NT = FULL + 1
STEPS = FULL * ROWS + LROWS
RING = 4
SCALAR_SHARE = (1, 2, 2, 1, 2, 2, 1, 2)
VC = D + 1
VCH = 120
EC = 500


def reversed_half(buf, b):
    a = buf[64:128, b, L - 1:L]
    return bass.AP(a.tensor, a.offset, [list(a.ap[0]), [-HALF, 2], [-1, HALF]])


def on_scalar(i, j):
    return j < SCALAR_SHARE[i % len(SCALAR_SHARE)]


def keep_warm(pe, bank, idle, count):
    for _ in range(count):
        pe.matmul(bank[:, 0:HALF], idle[:, 0, 0:128], idle[:, 1, 0:HALF], start=True, stop=True)


def build(nc, A, out):
    scratch_qk = nc.dram_tensor("scratch_qk", (B * HP, 128, L), F32, kind="Internal").ap()
    scratch_ks = nc.dram_tensor("scratch_ks", (NH * 3, TOK), BF16, kind="Internal").ap()
    scratch_v = nc.dram_tensor("scratch_v", (TOK, 2 * NH * D), F32, kind="Internal").ap()

    whole = ExitStack()
    with whole:
        def sbuf(ctx, name, shape, dt=F32):
            return ctx.enter_context(nc.sbuf_tensor(name, shape, dt))

        def psum(ctx, name, shape):
            return ctx.enter_context(nc.psum_tensor(name, shape, F32))

        def semaphore(ctx, name):
            return ctx.enter_context(nc.semaphore(name))

        hx = sbuf(whole, "hx", [CH, NC, D])
        of_acc = sbuf(whole, "of_acc", [CH, BC + NC, D])
        ob_acc = sbuf(whole, "ob_acc", [128, 1 + B, HALF])
        xt = sbuf(whole, "xt", [128, TOK])
        wkc = sbuf(whole, "wkc", [128, HP])
        ident = sbuf(whole, "ident", [128, 128])
        window = sbuf(whole, "window", [128, 62])
        select = sbuf(whole, "select", [6, 2, 128], BF16)
        vinit = sbuf(whole, "vinit", [128, 4])

        phase_tokens(nc, A, sbuf, psum, semaphore, hx, of_acc, ob_acc, ident, window, select, vinit, xt, wkc,
                     scratch_qk, scratch_ks, scratch_v)
        phase_attend(nc, sbuf, psum, semaphore, of_acc, ob_acc, ident, window, select, vinit, xt, wkc,
                     scratch_qk, scratch_ks, scratch_v)
        phase_feed(nc, A, out, sbuf, psum, semaphore, hx, of_acc, ob_acc, ident, xt)


def layernorm(nc, vec, link, src, mean, var, cen, sq, var_ready, std_ready, level):
    n, c = src.shape[0], src.shape[1]
    link(vec.reduce_sum(mean[:, :], src, axis=AX.X))
    link(vec.tensor_scalar(mean[:, :], mean[:, :], 1.0 / D, None, ALU.mult))
    link(vec.tensor_tensor(cen, src, mean[:, :].unsqueeze(2).to_broadcast([n, c, D]), ALU.subtract))
    link(vec.tensor_tensor(sq, cen, cen, ALU.mult))
    link(vec.reduce_sum(var[:, :], sq, axis=AX.X))
    vec.tensor_scalar(var[:, :], var[:, :], 1.0 / D, EPS, ALU.mult, ALU.add).then_inc(var_ready, 1)
    vec.wait_ge(std_ready, level)
    link(vec.reciprocal(var[:, :], var[:, :]))


def phase_tokens(nc, A, sbuf, psum, semaphore, hx, of_acc, ob_acc, ident, window, select, vinit, xt, wkc,
                 scratch_qk, scratch_ks, scratch_v):
    with ExitStack() as ctx:
        h1 = sbuf(ctx, "h1", [CH, NC, D])
        w1b = sbuf(ctx, "w1b", [10, 128])
        w2b = sbuf(ctx, "w2b", [128, 128])
        w4d = sbuf(ctx, "w4d", [128, D])
        w3b = sbuf(ctx, "w3b", [7, D])
        select32 = sbuf(ctx, "select32", [6, 2, 128])
        with ExitStack() as inner:
            x10 = sbuf(inner, "x10", [10, B, L])
            x7 = sbuf(inner, "x7", [7, TOK])
            state = sbuf(inner, "state", [128, B, L + 2])
            last = sbuf(inner, "last", [128, B, L + 2])
            ps = [psum(inner, f"ps{k}", [128, 2, 512]) for k in range(4)]
            loaded = semaphore(inner, "loaded")
            zeroed = semaphore(inner, "zeroed")
            idle_set = semaphore(inner, "idle_set")
            summed = semaphore(inner, "summed")
            kept_act = semaphore(inner, "kept_act")
            kept_vec = semaphore(inner, "kept_vec")
            mixed = semaphore(inner, "mixed")
            mixed_act = semaphore(inner, "mixed_act")
            mixed_vec = semaphore(inner, "mixed_vec")
            NLOAD = 10
            with nc.Block() as block:
                @block.sync
                def _(sp):
                    sp.dma_start(x10[:, :, :], A["x10"].rearrange("k (b l) -> k b l", b=B)).then_inc(loaded, 16)
                    sp.dma_start(w1b[:, :], A["w1b"]).then_inc(loaded, 16)
                    sp.dma_start(w2b[:, :], A["w2b"]).then_inc(loaded, 16)
                    sp.dma_start(w4d[:, :], A["w4d"]).then_inc(loaded, 16)
                    sp.dma_start(w3b[:, :], A["w3b"]).then_inc(loaded, 16)
                    sp.dma_start(x7[:, :], A["x7"]).then_inc(loaded, 16)
                    sp.dma_start(ident[:, :], A["ident"]).then_inc(loaded, 16)
                    sp.dma_start(window[:, :], A["window"]).then_inc(loaded, 16)
                    sp.dma_start(select32[:, :, :], A["select"].rearrange("r (a p) -> r a p", a=2)).then_inc(loaded, 16)
                    sp.dma_start(vinit[:, :], A["vinit"]).then_inc(loaded, 16)
                    sp.wait_ge(loaded, 16 * NLOAD)

                @block.gpsimd
                def _(pool):
                    pool.memset(ob_acc[:, 0:2, :], 0.0).then_inc(idle_set, 1)
                    pool.memset(state[:, :, 0:1], 0.0).then_inc(zeroed, 1)
                    pool.memset(last[:, :, 1:2], 0.0).then_inc(zeroed, 1)
                    pool.memset(last[:, :, L:L + 1], 0.0).then_inc(zeroed, 1)
                    pool.memset(of_acc[:, :, :], 0.0)
                    pool.memset(ob_acc[:, 2:, :], 0.0)

                @block.tensor
                def _(pe):
                    pe.wait_ge(idle_set, 1)
                    keep_warm(pe, ps[3][:, 0, :], ob_acc, 5)
                    pe.wait_ge(loaded, 16 * NLOAD)
                    pe.wait_ge(zeroed, 3)

                    def into(b, h):
                        return ps[b % 4][:, h, 0:HALF]

                    for b in range(B):
                        if b >= 4:
                            pe.wait_ge((kept_act, kept_vec)[b % 2], (b - 4) // 2 + 1)
                        for h in range(2):
                            mm = pe.matmul(into(b, h), w1b[:, :], x10[:, b, h * HALF:(h + 1) * HALF],
                                           start=True, stop=True)
                        mm.then_inc(summed, 1)
                    with pe.Fori(1, ROUNDS) as t:
                        for b0 in range(0, B, 4):
                            for b in range(b0, b0 + 4):
                                pe.wait_ge((kept_act, kept_vec)[b % 2], t * 4 + (b // 2 - 1))
                                for h in range(2):
                                    pe.matmul(into(b, h), w1b[:, :], x10[:, b, h * HALF:(h + 1) * HALF],
                                              start=True, stop=False)
                            for b in range(b0, b0 + 4):
                                pe.wait_ge((kept_act, kept_vec)[b % 2], t * 4 - 3 + b // 2)
                                for h in range(2):
                                    mm = pe.matmul(into(b, h), w2b[:, :], state[:, b, h * HALF:(h + 1) * HALF],
                                                   start=False, stop=True)
                                mm.then_inc(summed, 1)
                    pe.wait_ge(kept_act, 4 * ROUNDS)
                    pe.wait_ge(kept_vec, 4 * ROUNDS)
                    for g in range(NC // 8):
                        for k in range(8):
                            c = 8 * g + k
                            b, o = c // BC, 1 + CH * (c % BC)
                            dst = ps[g // 2][0:CH, g % 2, D * k:D * k + D]
                            pe.matmul(dst, last[:, b, o:o + CH], w4d[:, :], start=True, stop=False)
                            mm = pe.matmul(dst, x7[:, CH * c:CH * c + CH], w3b[:, :], start=False, stop=True)
                        mm.then_inc(mixed, 1)

                def two(buf, lo, p0=0, p1=128):
                    return lambda b: buf[p0:p1, b, lo:lo + L].rearrange("p (h c) -> p h c", h=2)

                @block.scalar
                def _(act):
                    act.wait_ge(zeroed, 3)
                    for b in range(0, B, 2):
                        act.wait_ge(summed, b + 1)
                        act.activation(two(state, 1)(b), ps[b % 4][:, :, 0:HALF], ACT.Relu).then_inc(kept_act, 1)
                    with act.Fori(1, ROUNDS - 1) as t:
                        for b in range(0, B, 2):
                            act.wait_ge(summed, t * B + b + 1)
                            act.activation(two(state, 1)(b), ps[b % 4][:, :, 0:HALF], ACT.Relu).then_inc(kept_act, 1)
                    for b in range(0, B, 2):
                        act.wait_ge(summed, (ROUNDS - 1) * B + b + 1)
                        act.activation(two(last, 2, 0, 64)(b), ps[b % 4][0:64, :, 0:HALF], ACT.Relu)
                        act.activation(reversed_half(last, b), ps[b % 4][64:128, :, 0:HALF],
                                       ACT.Relu).then_inc(kept_act, 1)
                    for g in range(0, NC // 8, 2):
                        act.wait_ge(mixed, g + 1)
                        act.activation(h1[:, 8 * g:8 * g + 8, :], ps[g // 2][0:CH, 0, :].rearrange("p (k d) -> p k d", k=8),
                                       ACT.Relu).then_inc(mixed_act, 1)

                @block.vector
                def _(vec):
                    vec.wait_ge(zeroed, 3)
                    vec.wait_ge(loaded, 16 * NLOAD)
                    vec.tensor_copy(select[:, :, :], select32[:, :, :])
                    for b in range(1, B, 2):
                        vec.wait_ge(summed, b + 1)
                        vec.tensor_scalar(two(state, 1)(b), ps[b % 4][:, :, 0:HALF], 0.0, None, ALU.max).then_inc(kept_vec, 1)
                    with vec.Fori(1, ROUNDS - 1) as t:
                        for b in range(1, B, 2):
                            vec.wait_ge(summed, t * B + b + 1)
                            vec.tensor_scalar(two(state, 1)(b), ps[b % 4][:, :, 0:HALF], 0.0, None,
                                              ALU.max).then_inc(kept_vec, 1)
                    for b in range(1, B, 2):
                        vec.wait_ge(summed, (ROUNDS - 1) * B + b + 1)
                        vec.tensor_scalar(two(last, 2, 0, 64)(b), ps[b % 4][0:64, :, 0:HALF], 0.0, None, ALU.max)
                        vec.tensor_scalar(reversed_half(last, b), ps[b % 4][64:128, :, 0:HALF], 0.0, None,
                                          ALU.max).then_inc(kept_vec, 1)
                    for g in range(1, NC // 8, 2):
                        vec.wait_ge(mixed, g + 1)
                        vec.tensor_scalar(h1[:, 8 * g:8 * g + 8, :],
                                          ps[g // 2][0:CH, 1, :].rearrange("p (k d) -> p k d", k=8),
                                          0.0, None, ALU.max).then_inc(mixed_vec, 1)

        with ExitStack() as inner:
            mean = sbuf(inner, "mean", [CH, NC])
            var = sbuf(inner, "var", [CH, NC])
            cen = sbuf(inner, "cen", [CH, NC, D])
            twice = sbuf(inner, "twice", [CH, NC, 2, D])
            w32 = sbuf(inner, "w32", [128, 3 * NH * D])
            wp = [sbuf(inner, f"wp{k}", [128, 3 * NH * D], BF16) for k in range(3)]
            x12 = sbuf(inner, "x12_b", [128, TOK], BF16)
            x13 = sbuf(inner, "x13_b", [128, TOK], BF16)
            bq = sbuf(inner, "bq", [128, HP])
            bv = sbuf(inner, "bv", [128, 2 * NH * D])
            wkt = sbuf(inner, "wkt", [D, NH])
            ks32 = twice[0:NH, :, :, :].rearrange("p c a d -> p (c a d)")[:, 0:TOK]
            qs = [sbuf(inner, f"qs{k}", [128, L]) for k in range(2)]
            vs = [sbuf(inner, f"vs{k}", [128, 2 * NH * D]) for k in range(3)]
            left = [vs[k][:, 0:L] for k in range(2)]
            vs.append(w32[:, 0:2 * NH * D])
            kparts = sbuf(inner, "kparts", [NH, 2, TOK], BF16)
            pt = [psum(inner, f"pt{k}", [128, 512]) for k in range(2)]
            pq = [psum(inner, f"pq{k}", [128, 2, 512]) for k in range(2)]
            pv = [psum(inner, f"pv{k}", [128, 512]) for k in range(2)]
            weights = semaphore(inner, "weights")
            chain = semaphore(inner, "chain_b")
            var_ready = semaphore(inner, "var_ready")
            std_ready = semaphore(inner, "std_ready")
            norm_ready = semaphore(inner, "norm_ready")
            twice_ready = semaphore(inner, "twice_ready")
            turned = semaphore(inner, "turned")
            xt_act = semaphore(inner, "xt_act")
            xt_vec = semaphore(inner, "xt_vec")
            ks_sum = semaphore(inner, "ks_sum")
            ks_kept = semaphore(inner, "ks_kept")
            part_act = semaphore(inner, "part_act")
            part_vec = semaphore(inner, "part_vec")
            q_sum = semaphore(inner, "q_sum")
            q_made = semaphore(inner, "q_made")
            w_split = semaphore(inner, "w_split")
            x_first = semaphore(inner, "x_first")
            x_left = semaphore(inner, "x_left")
            x_second = semaphore(inner, "x_second")
            x_split = semaphore(inner, "x_split")
            turn_b = semaphore(inner, "turn_b")
            q_stored = [semaphore(inner, f"q_stored{k}") for k in range(2)]
            v_sum = semaphore(inner, "v_sum")
            v_made = semaphore(inner, "v_made")
            NVS = len(vs)
            v_stored = [semaphore(inner, f"v_stored{k}") for k in range(NVS)]
            ks_stored = [semaphore(inner, f"ks_stored{k}") for k in range(3)]
            NV = TOK // VCH
            QCRED = 2 * HP + 2
            KS_AT = (4, 12)
            with nc.Block() as block:
                @block.sync
                def _(sp):
                    sp.dma_start(w32[:, :], A["wqv"]).then_inc(weights, 16)
                    sp.dma_start(bq[:, :], A["bq"]).then_inc(weights, 16)
                    sp.dma_start(bv[:, :], A["bv"].partition_broadcast(128)).then_inc(weights, 16)
                    sp.dma_start(wkc[:, :], A["wkc"]).then_inc(weights, 16)
                    sp.dma_start(wkt[:, :], A["wkt"]).then_inc(weights, 16)
                    parts = scratch_ks.rearrange("(h k) t -> h k t", k=3)
                    with sp.Fori(0, B) as b:
                        for p in range(HP):
                            n = b * HP + p
                            sp.wait_ge(q_made, n + (1 + QCRED))
                            sp.sem_inc(turn_b, 1)
                            sp.dma_start(scratch_qk[bass.ds(n, 1), :, :].rearrange("o p c -> (o p) c"),
                                         qs[p % 2][:, :]).then_inc(q_stored[p % 2], 16)
                    for c in range(NV):
                        sp.wait_ge(v_made, 2 * c + 2)
                        sp.dma_start(scratch_v[c * VCH:(c + 1) * VCH, :], vs[c % NVS][0:VCH, :]).then_inc(v_stored[c % NVS], 16)
                        if c % 10 == 9 and c // 10 < 3:
                            k = c // 10
                            sp.wait_ge(part_act, k + 1)
                            sp.dma_start(parts[:, k, :], kparts[:, k % 2, :]).then_inc(ks_stored[k], 16)
                    for k in range(2):
                        sp.wait_ge(q_stored[k], 8 * B * HP + 16)
                    for k in range(NVS):
                        sp.wait_ge(v_stored[k], 16 * len(range(k, NV, NVS)))
                    for k in range(3):
                        sp.wait_ge(ks_stored[k], 16)

                @block.tensor
                def _(pe):
                    pe.wait_ge(weights, 16 * 5)
                    pe.wait_ge(var_ready, 1)
                    keep_warm(pe, pv[0], ob_acc, 14)
                    pe.wait_ge(twice_ready, 1)
                    for g in range(NC // 4):
                        if g >= 2:
                            pe.wait_ge((xt_act, xt_vec)[g % 2], g // 2)
                        for k in range(4):
                            tr = pe.transpose(pt[g % 2][:, k * CH:(k + 1) * CH],
                                              twice[:, 4 * g + k, :, :].rearrange("p a d -> p (a d)"), ident[0:CH, 0:CH])
                        tr.then_inc(turned, 1)
                    keep_warm(pe, pv[0], ob_acc, 4)
                    pe.wait_ge(xt_act, NC // 8)
                    pe.wait_ge(xt_vec, NC // 8)
                    pe.wait_ge(w_split, 5)
                    with pe.Fori(0, B // 2) as g:
                        for r in range(2):
                            pe.wait_ge(x_split, g * 2 + (r + 1))
                            for p in range(HP):
                                n = g * (2 * HP) + (r * HP + p)
                                pe.wait_ge(q_made, n + QCRED - 1)
                                for h in range(2):
                                    for k, x in enumerate((x12, x12, x13)):
                                        mm = pe.matmul(pq[p % 2][:, h, 0:HALF], wp[k][:, p * 128:(p + 1) * 128],
                                                       x[:, bass.ds(g * (2 * L) + (r * L + h * HALF), HALF)],
                                                       start=(k == 0), stop=(k == 2))
                                mm.then_inc(q_sum, 1)
                    for k in range(2 * B):
                        if k >= 2:
                            pe.wait_ge(ks_kept, k - 1)
                        pe.matmul(pt[k % 2][0:NH, 0:HALF], wkt[:, :], xt[0:D, k * HALF:(k + 1) * HALF],
                                  start=True, stop=True).then_inc(ks_sum, 1)
                    for c in range(NV):
                        for h in range(2):
                            if c:
                                pe.wait_ge(v_made, 2 * c - 1 + h)
                            for k, x in enumerate((x12, x12, x13)):
                                mm = pe.matmul(pv[h][0:VCH, :], x[:, c * VCH:(c + 1) * VCH],
                                               wp[k][:, (1 + h) * 512:(2 + h) * 512], start=(k == 0), stop=(k == 2))
                            mm.then_inc(v_sum, 1)

                @block.gpsimd
                def _(pool):
                    pool.wait_ge(weights, 16 * 5)
                    pool.tensor_copy(wp[0][:, :], w32[:, :]).then_inc(w_split, 1)
                    pool.wait_ge(w_split, 1)
                    pool.tensor_tensor(w32[:, :], w32[:, :], wp[0][:, :], ALU.subtract).then_inc(w_split, 1)
                    pool.wait_ge(w_split, 2)
                    pool.tensor_copy(wp[2][64:128, :], wp[0][64:128, :]).then_inc(w_split, 1)
                    pool.wait_ge(w_split, 3)
                    pool.tensor_copy(wp[1][:, :], w32[:, :]).then_inc(w_split, 1)
                    pool.wait_ge(w_split, 4)
                    pool.tensor_tensor(wp[2][0:64, :], w32[0:64, :], wp[1][0:64, :], ALU.subtract).then_inc(w_split, 1)

                @block.scalar
                def _(act):
                    act.sem_inc(q_made, QCRED)
                    act.sem_inc(q_stored[0], 16)
                    act.sem_inc(q_stored[1], 16)
                    act.wait_ge(var_ready, 1)
                    act.activation(var[:, :], var[:, :], ACT.Sqrt).then_inc(std_ready, 1)
                    act.wait_ge(norm_ready, 1)
                    act.copy(twice[:, :, 1, :], twice[:, :, 0, :]).then_inc(twice_ready, 1)
                    for g in range(0, NC // 4, 2):
                        act.wait_ge(turned, g + 1)
                        act.copy(xt[:, 4 * CH * g:4 * CH * (g + 1)], pt[0][:, 0:4 * CH]).then_inc(xt_act, 1)
                    act.wait_ge(xt_act, NC // 8)
                    act.wait_ge(xt_vec, NC // 8)
                    for b in range(2):
                        act.copy(x12[:, b * L:(b + 1) * L], xt[:, b * L:(b + 1) * L]).then_inc(x_first, 1)
                    for b in range(B):
                        cols = slice(b * L, (b + 1) * L)
                        act.wait_ge(x_left, b + 1)
                        act.copy(x12[64:128, cols], left[b % 2][64:128, :])
                        act.copy(x13[0:64, cols], x12[0:64, cols]).then_inc(x_second, 1)
                        if b + 2 < B:
                            cols = slice((b + 2) * L, (b + 3) * L)
                            act.copy(x12[:, cols], xt[:, cols]).then_inc(x_first, 1)
                    act.wait_ge(ks_kept, 2 * B)
                    act.copy(kparts[:, 0, :], ks32[:, :]).then_inc(part_act, 1)
                    act.wait_ge(part_vec, 1)
                    act.copy(kparts[:, 1, :], ks32[:, :]).then_inc(part_act, 1)
                    act.wait_ge(part_vec, 2)
                    act.wait_ge(ks_stored[0], 16)
                    act.copy(kparts[:, 0, :], ks32[:, :]).then_inc(part_act, 1)

                @block.vector
                def _(vec):
                    links = [0]

                    def link(ins):
                        links[0] += 1
                        ins.then_inc(chain, 1)
                        vec.wait_ge(chain, links[0])

                    layernorm(nc, vec, link, h1[:, :, :], mean, var, cen[:, :, :], twice[:, :, 1, :], var_ready, std_ready, 1)
                    link(vec.tensor_tensor(twice[:, :, 0, :], cen[:, :, :],
                                           var[:, :].unsqueeze(2).to_broadcast([CH, NC, D]), ALU.mult))
                    vec.tensor_tensor(hx[:, :, :], h1[:, :, :], twice[:, :, 0, :], ALU.add).then_inc(norm_ready, 1)
                    for g in range(1, NC // 4, 2):
                        vec.wait_ge(turned, g + 1)
                        vec.tensor_copy(xt[:, 4 * CH * g:4 * CH * (g + 1)], pt[1][:, 0:4 * CH]).then_inc(xt_vec, 1)

                    def third(b):
                        cols = slice(b * L, (b + 1) * L)
                        vec.wait_ge(x_second, b + 1)
                        vec.tensor_tensor(x13[64:128, cols], left[b % 2][64:128, :], x12[64:128, cols],
                                          ALU.subtract).then_inc(x_split, 1)

                    for b in range(B):
                        cols = slice(b * L, (b + 1) * L)
                        if b >= 2:
                            vec.wait_ge(x_split, b - 1)
                        vec.wait_ge(x_first, b + 1)
                        vec.tensor_tensor(left[b % 2], xt[:, cols], x12[:, cols], ALU.subtract).then_inc(x_left, 1)
                        if b >= 1:
                            third(b - 1)
                    third(B - 1)
                    vec.wait_ge(x_split, B)
                    vec.wait_ge(weights, 16 * 5)
                    with vec.Fori(0, B) as b:
                        for p in range(HP):
                            n = b * HP + p
                            vec.wait_ge(q_stored[p % 2], b * (8 * HP) + (p // 2 + 1) * 16)
                            vec.wait_ge(q_sum, n + 1)
                            vec.tensor_scalar(qs[p % 2][:, :].rearrange("p (h c) -> p h c", h=2),
                                              pq[p % 2][:, :, 0:HALF], bq[:, p:p + 1], None,
                                              ALU.add).then_inc(q_made, 1)
                    for k in range(2 * B):
                        vec.wait_ge(ks_sum, k + 1)
                        vec.tensor_copy(ks32[:, k * HALF:(k + 1) * HALF], pt[k % 2][0:NH, 0:HALF]).then_inc(ks_kept, 1)
                    for c in range(NV):
                        if c == 3:
                            vec.wait_ge(w_split, 5)
                        if c >= NVS:
                            vec.wait_ge(v_stored[c % NVS], 16 * (c // NVS))
                        for h in range(2):
                            vec.wait_ge(v_sum, 2 * c + h + 1)
                            vec.tensor_tensor(vs[c % NVS][0:VCH, h * 512:(h + 1) * 512], pv[h][0:VCH, :],
                                              bv[0:VCH, h * 512:(h + 1) * 512], ALU.add).then_inc(v_made, 1)
                        if c in KS_AT:
                            k = KS_AT.index(c)
                            vec.wait_ge(part_act, k + 1)
                            vec.tensor_tensor(ks32[:, :], ks32[:, :], kparts[:, k, :], ALU.subtract).then_inc(part_vec, 1)


def phase_attend(nc, sbuf, psum, semaphore, of_acc, ob_acc, ident, window, select, vinit, xt, wkc,
                 scratch_qk, scratch_ks, scratch_v):
    with ExitStack() as ctx:
        ring = sbuf(ctx, "ring", [128, RING, QUADS, L])
        qk = [sbuf(ctx, f"qk{k}", [128, 3, L]) for k in range(2)]
        ksum = [sbuf(ctx, f"ksum{k}", [6, L], BF16) for k in range(2)]
        vb = [sbuf(ctx, f"vb{k}", [CH, BC, 2, D]) for k in range(2)]
        vbs = sbuf(ctx, "vbs", [CH, BC, 2, D])
        ex = [sbuf(ctx, f"ex{k}", [128, L]) for k in range(2)]
        ext = sbuf(ctx, "ext", [CH, BC, 2, L + 2])
        vf = [sbuf(ctx, f"vf{k}", [128, 2, VC]) for k in range(3)]
        zero = sbuf(ctx, "zero", [6, 512], BF16)
        rz = sbuf(ctx, "rz", [CH, BC, 2])
        part = sbuf(ctx, "part", [CH, BC, 2, D])
        sc = [psum(ctx, f"sc{k}", [128, 2, 512]) for k in range(2)]
        pv = psum(ctx, "pvf", [128, 2, 512])
        ob = psum(ctx, "ob", [128, 512])
        tr = psum(ctx, "tr", [128, 512])

        vset = semaphore(ctx, "vset")
        turn_c = semaphore(ctx, "turn_c")
        keys_made = semaphore(ctx, "keys_made")
        halves_made = semaphore(ctx, "halves_made")
        qk_in = [semaphore(ctx, f"qk_in{k}") for k in range(2)]
        vf_in = [semaphore(ctx, f"vf_in{k}") for k in range(3)]
        vf_used = semaphore(ctx, "vf_used")
        made_vec = semaphore(ctx, "made_vec")
        made_act = semaphore(ctx, "made_act")
        ring_free = semaphore(ctx, "ring_free")
        ex_made = semaphore(ctx, "ex_made")
        tr_made = semaphore(ctx, "tr_made")
        tr_kept = semaphore(ctx, "tr_kept")
        pv_free = semaphore(ctx, "pv_free")
        vbs_made = semaphore(ctx, "vbs_made")
        ob_made = semaphore(ctx, "ob_made")
        ob_free = semaphore(ctx, "ob_free")
        chain = semaphore(ctx, "chain_c")
        LINKS = 4

        def pairs(eng, body):
            with eng.Fori(0, B) as b:
                with eng.Fori(0, HP // 2) as g:
                    for par in range(2):
                        body(b * HP + g * 2 + par, b, g * 2 + par, par, b * (HP // 2) + g, b + (1 if par else g))

        def tiles(eng, n, body):
            body(n * NT + 1, 0, 0, n * STEPS, 0, "first")
            with eng.Fori(0, (FULL - 1) // 2) as u:
                for r in range(2):
                    t = u * 2 + (1 + r)
                    body(n * NT + t + 1, t, t * TILE, n * STEPS + t * ROWS, 1 - r, "inner")
            body(n * NT + FULL + 1, FULL, FULL * TILE, n * STEPS + FULL * ROWS, FULL % 2, "last")

        def members(kind):
            rows, count = (LROWS, LASTN) if kind == "last" else (ROWS, TILE)
            return [[(j, rows * j + i) for j in range(QUADS) if rows * j + i < count] for i in range(rows)]

        with nc.Block() as block:
            @block.sync
            def _(sp):
                sp.wait_ge(vset, 2)

                def tile(T, t, s0, G, par, kind, b, hp):
                    k = 2 if kind == "last" else par
                    sp.wait_ge(vf_used, T + 1)
                    sp.sem_inc(turn_c, 1)
                    rows = LROWS if kind == "last" else TILE
                    for j in range(QUADS if kind == "last" else 1):
                        cnt = min(rows, LASTN - rows * j) if kind == "last" else TILE
                        for h in range(2):
                            p0 = 32 * j + h
                            sp.dma_start(vf[k][p0:p0 + 2 * cnt - 1:2, h, 0:D],
                                         scratch_v[bass.ds(b * L + s0 + rows * j, cnt),
                                                   bass.ds(hp * 2 * D + h * D, D)]).then_inc(vf_in[k], 16)

                pairs(sp, lambda n, b, hp, par, m, back: tiles(sp, n, lambda *a: tile(*a, b, hp)))

            @block.gpsimd
            def _(pool):
                def load(n, b, hp, par, m, back):
                    pool.wait_ge(ob_made, n + 2)
                    pool.dma_start(qk[par][:, 1, :],
                                   scratch_qk[bass.ds(n, 1), :, :].rearrange("o p c -> (o p) c")).then_inc(qk_in[par], 16)
                    pool.dma_start(ksum[par][:, :],
                                   scratch_ks[bass.ds(hp * 6, 6), bass.ds(b * L, L)]).then_inc(qk_in[par], 16)
                    pool.dma_start(vb[par][:, :, :, :].rearrange("p c k d -> p c (k d)"),
                                   scratch_v[bass.ds(b * L, L), bass.ds(hp * 2 * D + NH * D, 2 * D)]
                                   .rearrange("(c p) d -> p c d", p=CH)).then_inc(qk_in[par], 16)

                pairs(pool, load)

            @block.tensor
            def _(pe):
                pe.wait_ge(vset, 2)

                def after(T, par, k, loads):
                    pe.wait_ge(ex_made, T + 1)
                    pe.wait_ge(vf_in[k], loads)
                    for c in range(BC):
                        mm = pe.matmul(pv[0:CH, c // 3, (c % 3) * 2 * VC:(c % 3 + 1) * 2 * VC],
                                       ex[par][:, c * CH:(c + 1) * CH],
                                       vf[k][:, :, :].rearrange("p k v -> p (k v)"),
                                       start=False, stop=(k == 2), skip_group_check=True)
                    mm.then_inc(vf_used, 1)

                def turn(T, par, r):
                    pe.wait_ge(tr_kept, T * 2 + r + 1)
                    for c in range(3):
                        x = pe.transpose(tr[0:CH, c * 128:(c + 1) * 128],
                                         ex[par][:, (3 * r + c) * CH:(3 * r + c + 1) * CH], ident[:, :])
                    x.then_inc(tr_made, 1)

                def backward(c, n):
                    if c == 0:
                        pe.wait_ge(vbs_made, n + 1)
                        pe.wait_ge(tr_kept, n * NT * 2 + 3)
                        pe.wait_ge(ob_free, n + 1)
                    for k in range(2):
                        for h in range(2):
                            mm = pe.matmul(ob[64 * h:64 * h + 64, 0:HALF], vbs[:, c, k, :],
                                           ext[:, c, k, h * HALF:(h + 1) * HALF],
                                           start=(c + k == 0), stop=(c == BC - 1 and k == 1))
                    if c == BC - 1:
                        mm.then_inc(ob_made, 1)

                def tile(T, G, par, kind, npar, before, behind):
                    bank = sc[par]
                    for h in range(2):
                        pe.matmul(bank[:, h, 0:HALF], select[:, int(kind == "last"), :],
                                  ksum[npar][:, h * HALF:(h + 1) * HALF],
                                  start=True, stop=False, skip_group_check=True)
                    steps = members(kind)
                    for i, js in enumerate(steps):
                        pe.wait_ge(made_vec, G + i + 1)
                        pe.wait_ge(made_act, G + i + 1)
                        for h in range(2):
                            for j, s in js:
                                mm = pe.matmul(bank[32 * j:32 * j + 32, h, 0:HALF], window[:, 30 - 2 * i:62 - 2 * i],
                                               ring[:, i % RING, j, h * HALF:(h + 1) * HALF],
                                               start=False, stop=(i == len(steps) - 1 or (j, s + 1) == (QUADS - 1, LASTN)),
                                               skip_group_check=True)
                        mm.then_inc(ring_free, 1)
                        if i == 4:
                            after(*before)
                        if i in (5, 8):
                            turn(before[0], before[1], i // 8)
                        if behind is not None and i >= ROWS - BC:
                            backward(i - (ROWS - BC), behind)

                def open_sums():
                    for g in range(2):
                        pe.matmul(pv[0:CH, g, 0:3 * 2 * VC], zero[:, 0:CH], zero[:, 0:3 * 2 * VC],
                                  start=True, stop=False, skip_group_check=True)

                def pair(n, b, hp, npar, m, back):
                    pe.wait_ge(qk_in[npar], (m + 1) * 48)
                    tile(n * NT + 1, n * STEPS, 0, "first", npar,
                         (n * NT, FULL % 2, 2, n * 16 * 2 * QUADS + 16), n)
                    pe.wait_ge(pv_free, n + 1)
                    open_sums()
                    with pe.Fori(0, (FULL - 1) // 2) as u:
                        for r in range(2):
                            T = n * NT + (u * 2 + (2 + r))
                            tile(T, n * STEPS + u * (2 * ROWS) + (1 + r) * ROWS, 1 - r, "inner", npar,
                                 (T - 1, r, r, (n * (6 - r) + u + 1) * 32), None)
                    T = n * NT + FULL + 1
                    tile(T, n * STEPS + FULL * ROWS, FULL % 2, "last", npar, (T - 1, 0, 0, (n * 6 + 6) * 32), None)

                open_sums()
                for h in range(2):
                    mm = pe.matmul(sc[FULL % 2][:, h, 0:HALF], zero[:, 0:128], zero[:, 0:HALF], start=True, stop=True)
                mm.then_inc(ring_free, RING)
                pairs(pe, pair)
                N = B * HP
                after(N * NT, FULL % 2, 2, N * 16 * 2 * QUADS + 16)
                for r in range(2):
                    turn(N * NT, FULL % 2, r)
                for c in range(BC):
                    backward(c, N)

            def keep_half(copy, r, s0, kind):
                src = tr[0:CH, 0:384].rearrange("p (c m k) -> p c m k", c=3, k=2)
                if kind == "last":
                    for k in range(2):
                        for c in range(3):
                            dst = ext[:, 3 * r + c, k, FULL * TILE:FULL * TILE + QUADS * LROWS]
                            x = copy(dst.rearrange("p (j i) -> p j i", j=QUADS),
                                     src[:, c, :, k].rearrange("p (j i) -> p j i", j=QUADS)[:, :, 0:LROWS])
                    return x
                for k in range(2):
                    x = copy(ext[:, 3 * r:3 * r + 3, k, bass.ds(s0, TILE)], src[:, :, :, k])
                return x

            @block.scalar
            def _(act):
                act.sem_inc(ob_made, 2)
                act.sem_inc(vf_used, 2)
                act.sem_inc(vf_in[2], 16)
                act.sem_inc(tr_kept, 1)
                act.sem_inc(ob_free, 1)

                def finish(par):
                    act.activation(ex[par][:, :].rearrange("p (h c) -> p h c", h=2), sc[par][:, :, 0:HALF],
                                   ACT.Exp, scale=-2.0 / D ** 0.5).then_inc(ex_made, 1)

                def keep(T, s0, kind):
                    act.wait_ge(tr_made, T * 2 + 2)
                    keep_half(act.copy, 1, s0, kind).then_inc(tr_kept, 1)

                def tile(T, s0, G, par, kind, npar, before):
                    rows = members(kind)
                    for i, js in enumerate(rows):
                        act.wait_ge(ring_free, G + i + 1)
                        for j, s in js:
                            if on_scalar(i, j):
                                x = act.activation(ring[:, i % RING, j, :], qk[npar][:, 0, :], ACT.Abs,
                                                   bias=qk[npar][:, 2, bass.ds(s0 + s, 1)], scale=0.5)
                        x.then_inc(made_act, 1)
                        if i == RING - 1:
                            finish(1 - par)
                        if i == min(12, len(rows) - 1):
                            keep(*before)

                def pair(n, b, hp, npar, m, back):
                    act.wait_ge(qk_in[npar], (m + 1) * 48)
                    act.mul(qk[npar][:, 2, :], qk[npar][:, 1, :], -0.5).then_inc(halves_made, 1)
                    act.wait_ge(halves_made, n + 1)
                    act.wait_ge(keys_made, n + 1)
                    tile(n * NT + 1, 0, n * STEPS, 0, "first", npar, (n * NT, FULL * TILE, "last"))
                    with act.Fori(0, (FULL - 1) // 2) as u:
                        for r in range(2):
                            t = u * 2 + (1 + r)
                            T = n * NT + t + 1
                            tile(T, t * TILE, n * STEPS + t * ROWS, 1 - r, "inner", npar,
                                 (T - 1, (t - 1) * TILE, "inner"))
                    T = n * NT + FULL + 1
                    tile(T, FULL * TILE, n * STEPS + FULL * ROWS, FULL % 2, "last", npar,
                         (T - 1, (FULL - 1) * TILE, "inner"))

                pairs(act, pair)
                N = B * HP
                act.wait_ge(ring_free, N * STEPS + RING)
                finish(FULL % 2)
                keep(N * NT, FULL * TILE, "last")

            @block.vector
            def _(vec):
                vec.memset(zero[:, :], 0.0)
                vec.memset(vb[1][:, :, :, :], 0.0)
                vec.memset(ext[:, :, :, :], 0.0)
                for k in range(3):
                    x = vec.memset(vf[k][:, :, :], 0.0)
                x.then_inc(vset, 1)
                vec.wait_ge(vset, 1)
                for k in range(3):
                    x = vec.tensor_copy(vf[k][:, :, D:VC].rearrange("p h o -> p (h o)"),
                                        vinit[:, 2 * (k // 2):2 * (k // 2) + 2])
                x.then_inc(vset, 1)

                def keep(T, s0, kind):
                    vec.wait_ge(tr_made, T * 2 + 1)
                    keep_half(vec.tensor_copy, 0, s0, kind).then_inc(tr_kept, 1)

                def link(ins, level):
                    ins.then_inc(chain, 1)
                    vec.wait_ge(chain, level)

                def weigh(n, npar):
                    vec.wait_ge(vf_used, n * NT + 3)
                    for g in range(2):
                        sums = pv[0:CH, g, 0:3 * 2 * VC].rearrange("p (c k v) -> p c k v", c=3, k=2)
                        x = vec.tensor_scalar(rz[:, 3 * g:3 * g + 3, :].unsqueeze(3), sums[:, :, :, D:VC], 1.0, None, ALU.add)
                    link(x, n * LINKS + 1)
                    link(vec.reciprocal(rz[:, :, :], rz[:, :, :]), n * LINKS + 2)
                    vec.tensor_tensor(vbs[:, :, :, :].rearrange("p c k d -> p (c k) d"),
                                      vb[npar][:, :, :, :].rearrange("p c k d -> p (c k) d"),
                                      rz[:, :, :].rearrange("p c k -> p (c k)").unsqueeze(2)
                                      .to_broadcast([CH, 2 * BC, D]), ALU.mult).then_inc(vbs_made, 1)

                def forward(n, back):
                    for g in range(2):
                        for k in range(2):
                            sums = pv[0:CH, g, 0:3 * 2 * VC].rearrange("p (c k v) -> p c k v", c=3, k=2)
                            x = vec.tensor_tensor(part[:, 3 * g:3 * g + 3, k, :], sums[:, :, k, 0:D],
                                                  rz[:, 3 * g:3 * g + 3, k].unsqueeze(2).to_broadcast([CH, 3, D]), ALU.mult)
                    x.then_inc(pv_free, 1)
                    vec.wait_ge(pv_free, n + 1)
                    mine = of_acc[:, bass.ds(back * BC, BC), :]
                    link(vec.tensor_tensor(mine, mine, part[:, :, 0, :], ALU.add), n * LINKS + 3)
                    link(vec.tensor_tensor(mine, mine, part[:, :, 1, :], ALU.add), n * LINKS + 4)

                def backward(n, back):
                    vec.wait_ge(ob_made, n + 3)
                    vec.wait_ge(ob_free, n + 1)
                    mine = ob_acc[:, bass.ds(back, 1), :].rearrange("p o c -> p (o c)")
                    vec.tensor_tensor(mine, mine, ob[:, 0:HALF], ALU.add).then_inc(ob_free, 1)

                def tile(s0, G, kind, npar, before, behind):
                    for i, js in enumerate(members(kind)):
                        vec.wait_ge(ring_free, G + i + 1)
                        for j, s in js:
                            if not on_scalar(i, j):
                                x = vec.tensor_scalar(ring[:, i % RING, j, :], qk[npar][:, 0, :],
                                                      qk[npar][:, 1, bass.ds(s0 + s, 1)],
                                                      qk[npar][:, 2, bass.ds(s0 + s, 1)], ALU.max, ALU.add)
                        x.then_inc(made_vec, 1)
                        if i == 9:
                            keep(*before)
                            if behind:
                                weigh(behind[0], 1 - npar)
                        if behind and i == 11:
                            forward(*behind)

                def pair(n, b, hp, npar, m, back):
                    vec.wait_ge(qk_in[npar], (m + 1) * 48)
                    vec.tensor_scalar(qk[npar][:, 0, :], xt[:, bass.ds(b * L, L)], wkc[:, bass.ds(hp, 1)], None,
                                      ALU.mult).then_inc(keys_made, 1)
                    vec.wait_ge(keys_made, n + 1)
                    vec.wait_ge(halves_made, n + 1)
                    tile(0, n * STEPS, "first", npar, (n * NT, FULL * TILE, "last"), (n, back))
                    with vec.Fori(0, (FULL - 1) // 2) as u:
                        for r in range(2):
                            t = u * 2 + (1 + r)
                            tile(t * TILE, n * STEPS + t * ROWS, "inner", npar,
                                 (n * NT + t, (t - 1) * TILE, "inner"), None)
                    tile(FULL * TILE, n * STEPS + FULL * ROWS, "last", npar,
                         (n * NT + FULL, (FULL - 1) * TILE, "inner"), None)
                    backward(n, back)

                pairs(vec, pair)
                N = B * HP
                keep(N * NT, FULL * TILE, "last")
                weigh(N, (N - 1) % 2)
                forward(N, B)
                backward(N, B)


def phase_feed(nc, A, out, sbuf, psum, semaphore, hx, of_acc, ob_acc, ident, x2t):
    with ExitStack() as ctx:
        h2 = sbuf(ctx, "h2", [CH, NC, D])
        wgt = sbuf(ctx, "wgt", [D, NE])
        bg = sbuf(ctx, "bg", [CH, NE])
        tri = sbuf(ctx, "tri", [CH, NE, NE])
        w1t = sbuf(ctx, "w1t", [128, 2 * NE, 128])
        w1p = [sbuf(ctx, f"w1p{k}", [128, 2 * NE, 128], BF16) for k in range(3)]
        b1c = sbuf(ctx, "b1c", [128, 2 * NE])
        w2t = sbuf(ctx, "w2t", [128, NE, 2, D])
        b2 = sbuf(ctx, "b2", [CH, NE, D])
        comb = sbuf(ctx, "comb", [CH, NC, NE])
        gs = sbuf(ctx, "gs", [CH, NC, NE])
        gmax = sbuf(ctx, "gmax", [CH, NC])
        gsum = sbuf(ctx, "gsum", [CH, NC])
        gex = sbuf(ctx, "gex", [CH, NC, NE])
        rank = sbuf(ctx, "rank", [CH, NC, NE])
        big = sbuf(ctx, "big", [CH, NC // 2, NE, NE])
        eqs = sbuf(ctx, "eqs", [CH, NC // 2, NE, NE])
        weights = semaphore(ctx, "weights_d")
        scored = semaphore(ctx, "scored")
        w1_split = semaphore(ctx, "w1_split")
        NW = 9
        with ExitStack() as inner:
            o = sbuf(inner, "o", [CH, NC, D])
            sg = sbuf(inner, "sg", [CH, NC, D])
            cen = sbuf(inner, "cen_d", [CH, NC, D])
            twice = sbuf(inner, "twice_d", [CH, NC, 2, D])
            gt = sbuf(inner, "gt", [D, TOK])
            fant = sbuf(inner, "fant", [D, D])
            fb = sbuf(inner, "fb", [CH, D])
            mean = sbuf(inner, "mean_d", [CH, NC])
            var = sbuf(inner, "var_d", [CH, NC])
            pa = [psum(inner, f"pa{k}", [128, 512]) for k in range(7)]
            pg = psum(inner, "pg", [128, 512])
            chain = semaphore(inner, "chain_d")
            back_t = semaphore(inner, "back_t")
            o_made = semaphore(inner, "o_made")
            sg_made = semaphore(inner, "sg_made")
            g_made = semaphore(inner, "g_made")
            g_turned = semaphore(inner, "g_turned")
            gt_act = semaphore(inner, "gt_act")
            gt_vec = semaphore(inner, "gt_vec")
            y_sum = semaphore(inner, "y_sum")
            var_ready = semaphore(inner, "var_ready_d")
            std_ready = semaphore(inner, "std_ready_d")
            norm_ready = semaphore(inner, "norm_ready_d")
            twice_ready = semaphore(inner, "twice_ready_d")
            turned = semaphore(inner, "turned_d")
            xt_act = semaphore(inner, "xt_act_d")
            xt_vec = semaphore(inner, "xt_vec_d")
            gate_sum = semaphore(inner, "gate_sum")
            with nc.Block() as block:
                @block.sync
                def _(sp):
                    sp.dma_start(fant[:, :], A["fant"]).then_inc(weights, 16)
                    sp.dma_start(fb[:, :], A["fb"].partition_broadcast(CH)).then_inc(weights, 16)
                    sp.dma_start(wgt[:, :], A["wgt"]).then_inc(weights, 16)
                    sp.dma_start(bg[:, :], A["bg"].partition_broadcast(CH)).then_inc(weights, 16)
                    sp.dma_start(tri[:, :, :].rearrange("p a b -> p (a b)"),
                                 A["tri"].partition_broadcast(CH)).then_inc(weights, 16)
                    sp.dma_start(w1t[:, :, :].rearrange("p e m -> p (e m)"), A["w1t"]).then_inc(weights, 16)
                    sp.dma_start(b1c[:, :], A["b1c"]).then_inc(weights, 16)
                    sp.dma_start(w2t[:, :, :, :].rearrange("p e h d -> p (e h d)"), A["w2t"]).then_inc(weights, 16)
                    sp.dma_start(b2[:, :, :].rearrange("p e d -> p (e d)"),
                                 A["b2"].partition_broadcast(CH)).then_inc(weights, 16)
                    sp.wait_ge(weights, 16 * NW)

                @block.gpsimd
                def _(pool):
                    pool.wait_ge(weights, 16 * NW)
                    pool.tensor_copy(w1p[0][:, :, :], w1t[:, :, :]).then_inc(w1_split, 1)
                    pool.wait_ge(w1_split, 1)
                    pool.tensor_tensor(w1t[:, :, :], w1t[:, :, :], w1p[0][:, :, :], ALU.subtract).then_inc(w1_split, 1)
                    pool.wait_ge(w1_split, 2)
                    pool.tensor_copy(w1p[2][64:128, :, :], w1p[0][64:128, :, :]).then_inc(w1_split, 1)
                    pool.wait_ge(w1_split, 3)
                    pool.tensor_copy(w1p[1][:, :, :], w1t[:, :, :]).then_inc(w1_split, 1)
                    pool.wait_ge(w1_split, 4)
                    pool.tensor_tensor(w1p[2][0:64, :, :], w1t[0:64, :, :], w1p[1][0:64, :, :],
                                       ALU.subtract).then_inc(w1_split, 1)

                @block.tensor
                def _(pe):
                    for g in range(B):
                        h = g // (B // 2)
                        for k in range(2 * 3):
                            b, q = 2 * (g % (B // 2)) + k // 3, k % 3
                            mm = pe.transpose((pa + [pg])[g][0:CH, D * k:D * k + D],
                                              ob_acc[64 * h:64 * h + 64, 1 + b, q * CH:(q + 1) * CH],
                                              ident[64 * h:64 * h + 64, 64 * h:64 * h + 64])
                        mm.then_inc(back_t, 1)
                    pe.wait_ge(o_made, 1)
                    keep_warm(pe, pa[6], ob_acc, 9)
                    pe.wait_ge(g_made, 1)
                    for g in range(NC // 4):
                        if g >= 2:
                            pe.wait_ge((gt_act, gt_vec)[g % 2], g // 2)
                        for k in range(4):
                            mm = pe.transpose(pa[g % 2][0:D, k * CH:(k + 1) * CH], sg[:, 4 * g + k, :], ident[0:CH, 0:CH])
                        mm.then_inc(g_turned, 1)
                    pe.wait_ge(weights, 16 * NW)
                    pe.wait_ge(gt_act, NC // 8)
                    pe.wait_ge(gt_vec, NC // 8)
                    for g in range(NC // 8):
                        for k in range(8):
                            c = 8 * g + k
                            mm = pe.matmul(pa[g][0:CH, D * k:D * k + D], gt[:, c * CH:(c + 1) * CH], fant[:, :],
                                           start=True, stop=True)
                        mm.then_inc(y_sum, 1)
                    pe.wait_ge(var_ready, 1)
                    keep_warm(pe, pa[6], ob_acc, 12)
                    pe.wait_ge(twice_ready, 1)
                    for g in range(NC // 4):
                        if g >= 2:
                            pe.wait_ge((xt_act, xt_vec)[g % 2], g // 2)
                        for k in range(4):
                            mm = pe.transpose(pa[g % 2][:, k * CH:(k + 1) * CH],
                                              twice[:, 4 * g + k, :, :].rearrange("p a d -> p (a d)"), ident[0:CH, 0:CH])
                        mm.then_inc(turned, 1)
                    pe.wait_ge(xt_act, NC // 8)
                    pe.wait_ge(xt_vec, NC // 8)
                    for c in range(NC):
                        mm = pe.matmul(pg[0:CH, NE * c:NE * c + NE], x2t[0:D, c * CH:(c + 1) * CH], wgt[:, :],
                                       start=True, stop=True)
                    mm.then_inc(gate_sum, 1)

                @block.scalar
                def _(act):
                    act.wait_ge(o_made, 1)
                    act.activation(sg[:, :, :], o[:, :, :], ACT.Sigmoid, scale=1.702).then_inc(sg_made, 1)
                    for g in range(0, NC // 4, 2):
                        act.wait_ge(g_turned, g + 1)
                        act.copy(gt[:, 4 * CH * g:4 * CH * (g + 1)], pa[0][0:D, 0:4 * CH]).then_inc(gt_act, 1)
                    act.wait_ge(var_ready, 1)
                    act.activation(var[:, :], var[:, :], ACT.Sqrt).then_inc(std_ready, 1)
                    act.wait_ge(norm_ready, 1)
                    act.copy(twice[:, :, 1, :], twice[:, :, 0, :]).then_inc(twice_ready, 1)
                    for g in range(0, NC // 4, 2):
                        act.wait_ge(turned, g + 1)
                        act.copy(x2t[:, 4 * CH * g:4 * CH * (g + 1)], pa[0][:, 0:4 * CH]).then_inc(xt_act, 1)

                @block.vector
                def _(vec):
                    links = [0]

                    def link(ins):
                        links[0] += 1
                        ins.then_inc(chain, 1)
                        vec.wait_ge(chain, links[0])

                    halves = [buf.rearrange("p (b h q) d -> p b h q d", b=B, h=2) for buf in (o[:, :, :], of_acc[:, BC:, :])]
                    for g in range(B):
                        vec.wait_ge(back_t, g + 1)
                        h, b = g // (B // 2), 2 * (g % (B // 2))
                        x = vec.tensor_tensor(halves[0][:, b:b + 2, h, :, :], halves[1][:, b:b + 2, h, :, :],
                                              (pa + [pg])[g][0:CH, 0:6 * D].rearrange("p (b q d) -> p b q d", b=2, q=3),
                                              ALU.add)
                    x.then_inc(o_made, 1)
                    vec.wait_ge(sg_made, 1)
                    vec.wait_ge(o_made, 1)
                    vec.tensor_tensor(sg[:, :, :], o[:, :, :], sg[:, :, :], ALU.mult).then_inc(g_made, 1)
                    for g in range(1, NC // 4, 2):
                        vec.wait_ge(g_turned, g + 1)
                        vec.tensor_copy(gt[:, 4 * CH * g:4 * CH * (g + 1)], pa[1][0:D, 0:4 * CH]).then_inc(gt_vec, 1)
                    vec.wait_ge(weights, 16 * NW)
                    link(vec.tensor_tensor(hx[:, :, :], hx[:, :, :],
                                           fb[:, :].unsqueeze(1).to_broadcast([CH, NC, D]), ALU.add))
                    for g in range(NC // 8):
                        vec.wait_ge(y_sum, g + 1)
                        x = vec.tensor_tensor(h2[:, 8 * g:8 * g + 8, :], hx[:, 8 * g:8 * g + 8, :],
                                              pa[g][0:CH, :].rearrange("p (k d) -> p k d", k=8), ALU.add)
                    link(x)
                    layernorm(nc, vec, link, h2[:, :, :], mean, var, cen[:, :, :], o[:, :, :], var_ready, std_ready, 1)
                    vec.tensor_tensor(twice[:, :, 0, :], cen[:, :, :],
                                      var[:, :].unsqueeze(2).to_broadcast([CH, NC, D]), ALU.mult).then_inc(norm_ready, 1)
                    for g in range(1, NC // 4, 2):
                        vec.wait_ge(turned, g + 1)
                        vec.tensor_copy(x2t[:, 4 * CH * g:4 * CH * (g + 1)], pa[1][:, 0:4 * CH]).then_inc(xt_vec, 1)
                    vec.wait_ge(gate_sum, 1)
                    vec.tensor_tensor(gs[:, :, :], pg[0:CH, 0:NC * NE].rearrange("p (c e) -> p c e", e=NE),
                                           bg[:, :].unsqueeze(1).to_broadcast([CH, NC, NE]), ALU.add).then_inc(scored, 1)

        with ExitStack() as inner:
            xc = sbuf(inner, "xc", [128, EC])
            x12 = [sbuf(inner, f"x12_{r}", [128, EC], BF16) for r in range(2)]
            x13 = [sbuf(inner, f"x13_{r}", [128, EC], BF16) for r in range(2)]
            hid = [[sbuf(inner, f"hid{r}_{k}", [128, EC]) for k in range(2 * NE)] for r in range(2)]
            wy = [sbuf(inner, f"wy{k}", [CH, NE, D]) for k in range(2)]
            red = [sbuf(inner, f"red{k}", [CH, D]) for k in range(2)]
            res = [sbuf(inner, f"res{k}", [CH, EC // CH, D]) for k in range(2)]
            pu = [psum(inner, f"pu{k}", [128, 512]) for k in range(4)]
            py = [psum(inner, f"py{k}", [128, 512]) for k in range(4)]
            xc_split = semaphore(inner, "xc_split")
            turn_p = semaphore(inner, "turn_p")
            XS = 6
            up = semaphore(inner, "up")
            relu_act = semaphore(inner, "relu_act")
            down = semaphore(inner, "down")
            y_free = semaphore(inner, "y_free")
            chain = semaphore(inner, "chain_e")
            gate_chain = semaphore(inner, "gate_chain")
            shifted = semaphore(inner, "shifted")
            gexp = semaphore(inner, "gexp")
            res_made = semaphore(inner, "res_made")
            turn_e = semaphore(inner, "turn_e")
            res_out = [semaphore(inner, f"res_out{k}") for k in range(2)]
            NQ = TOK // EC
            SUB = EC // CH
            view = out.rearrange("b t d -> (b t) d")
            LK = 2 * SUB
            with nc.Block() as block:
                @block.sync
                def _(sp):
                    with sp.Fori(0, NQ // 2) as it:
                        for r in range(2):
                            q = it * 2 + r
                            sp.wait_ge(res_made, q + 1)
                            sp.sem_inc(turn_e, 1)
                            sp.dma_start(view[bass.ds(q * EC, EC), :].rearrange("(c p) d -> p c d", p=CH),
                                         res[r][:, :, :]).then_inc(res_out[r], 16)
                    for r in range(2):
                        sp.wait_ge(res_out[r], 8 * NQ + 16)

                @block.gpsimd
                def _(pool):
                    with pool.Fori(0, NQ // 2) as it:
                        for r in range(2):
                            q = it * 2 + r
                            pool.wait_ge(up, q * (2 * NE) + 2 * NE)
                            at = [0]

                            def link(ins):
                                at[0] += 1
                                ins.then_inc(xc_split, 1)
                                pool.wait_ge(xc_split, q * XS + at[0])
                                pool.sem_inc(turn_p, 1)

                            link(pool.tensor_copy(xc[:, :], x2t[:, bass.ds(q * EC, EC)]))
                            link(pool.tensor_copy(x12[r][:, :], xc[:, :]))
                            link(pool.tensor_tensor(xc[:, :], xc[:, :], x12[r][:, :], ALU.subtract))
                            link(pool.tensor_copy(x13[r][0:64, :], x12[r][0:64, :]))
                            link(pool.tensor_copy(x12[r][64:128, :], xc[64:128, :]))
                            link(pool.tensor_tensor(x13[r][64:128, :], xc[64:128, :], x12[r][64:128, :], ALU.subtract))

                @block.tensor
                def _(pe):
                    def ups(q, r):
                        pe.wait_ge(xc_split, q * XS + XS)
                        for e in range(NE):
                            pe.wait_ge(relu_act, q * (2 * NE) + (2 * e + 2))
                            for h in range(2):
                                for k, x in enumerate((x12[r], x12[r], x13[r])):
                                    mm = pe.matmul(pu[(2 * e + h) % 4][:, 0:EC], w1p[k][:, 2 * e + h, :], x[:, :],
                                                   start=(k == 0), stop=(k == 2))
                                mm.then_inc(up, 1)

                    def downs(q, r):
                        pe.wait_ge(relu_act, q * (2 * NE) + (2 * NE + 4))
                        for s in range(SUB):
                            pe.wait_ge(y_free, q * SUB + (s + 1))
                            for e in range(NE):
                                for h in range(2):
                                    mm = pe.matmul(py[s][0:CH, e * D:(e + 1) * D],
                                                   hid[r][2 * e + h][:, s * CH:(s + 1) * CH], w2t[:, e, h, :],
                                                   start=(h == 0), stop=(h == 1))
                            mm.then_inc(down, 1)

                    pe.wait_ge(w1_split, 5)
                    with pe.Fori(0, NQ // 2) as it:
                        for r in range(2):
                            ups(it * 2 + r, r)
                            downs(it * 2 + r, r)

                @block.scalar
                def _(act):
                    act.wait_ge(shifted, 1)
                    act.activation(gex[:, :, :], gex[:, :, :], ACT.Exp).then_inc(gexp, 1)
                    act.sem_inc(up, 4 * NE)
                    act.sem_inc(relu_act, 4)
                    act.sem_inc(y_free, 4)
                    act.sem_inc(res_out[0], 16)
                    act.sem_inc(res_out[1], 16)
                    with act.Fori(0, NQ // 2) as it:
                        for r in range(2):
                            q = it * 2 + r
                            act.wait_ge(y_free, q * SUB + 1)
                            for k in range(2 * NE):
                                act.wait_ge(up, q * (2 * NE) + (k + 1 + 4 * NE))
                                act.activation(hid[r][k][:, :], pu[k % 4][:, 0:EC], ACT.Relu,
                                               bias=b1c[:, k:k + 1]).then_inc(relu_act, 1)

                @block.vector
                def _(vec):
                    links = [0]

                    def link_one(ins):
                        links[0] += 1
                        ins.then_inc(gate_chain, 1)
                        vec.wait_ge(gate_chain, links[0])

                    vec.wait_ge(scored, 1)
                    link_one(vec.reduce_max(gmax[:, :], gs[:, :, :], axis=AX.X))
                    vec.tensor_tensor(gex[:, :, :], gs[:, :, :], gmax[:, :].unsqueeze(2).to_broadcast([CH, NC, NE]),
                                      ALU.subtract).then_inc(shifted, 1)
                    for half in range(2):
                        cs = slice(half * NC // 2, (half + 1) * NC // 2)
                        n2 = NC // 2
                        for e in range(NE):
                            me = gs[:, cs, e:e + 1].to_broadcast([CH, n2, NE])
                            vec.tensor_tensor(big[:, :, e, :], gs[:, cs, :], me, ALU.is_gt)
                            x = vec.tensor_tensor(eqs[:, :, e, :], gs[:, cs, :], me, ALU.is_equal)
                        link_one(x)
                        link_one(vec.tensor_tensor(eqs[:, :, :, :].rearrange("p c a b -> p c (a b)"),
                                               eqs[:, :, :, :].rearrange("p c a b -> p c (a b)"),
                                               tri[:, :, :].rearrange("p a b -> p (a b)").unsqueeze(1)
                                               .to_broadcast([CH, n2, NE * NE]), ALU.mult))
                        link_one(vec.tensor_tensor(big[:, :, :, :].rearrange("p c a b -> p (c a b)"),
                                               big[:, :, :, :].rearrange("p c a b -> p (c a b)"),
                                               eqs[:, :, :, :].rearrange("p c a b -> p (c a b)"), ALU.add))
                        link_one(vec.reduce_sum(rank[:, cs, :].rearrange("p c e -> p (c e)"),
                                            big[:, :, :, :].rearrange("p c a b -> p (c a) b"), axis=AX.X))
                    link_one(vec.tensor_scalar(rank[:, :, :], rank[:, :, :], 1.5, None, ALU.is_lt))
                    vec.wait_ge(gexp, 1)
                    link_one(vec.tensor_tensor(gex[:, :, :], gex[:, :, :], rank[:, :, :], ALU.mult))
                    link_one(vec.reduce_sum(gsum[:, :], gex[:, :, :], axis=AX.X))
                    link_one(vec.reciprocal(gsum[:, :], gsum[:, :]))
                    link_one(vec.tensor_tensor(comb[:, :, :], gex[:, :, :],
                                           gsum[:, :].unsqueeze(2).to_broadcast([CH, NC, NE]), ALU.mult))

                    with vec.Fori(0, NQ // 2) as it:
                        for r in range(2):
                            q = it * 2 + r
                            at = [0]

                            def link(ins):
                                at[0] += 1
                                ins.then_inc(chain, 1)
                                vec.wait_ge(chain, q * LK + at[0])

                            vec.wait_ge(res_out[r], it * 16 + 16)
                            for s in range(SUB):
                                vec.wait_ge(down, q * SUB + (s + 1))
                                w = wy[s % 2]
                                x = vec.tensor_tensor(w[:, :, :], py[s][0:CH, :].rearrange("p (e d) -> p e d", e=NE),
                                                      b2[:, :, :], ALU.add)
                                x.then_inc(y_free, 1)
                                vec.wait_ge(y_free, q * SUB + (s + 5))
                                link(vec.tensor_tensor(w[:, :, :], w[:, :, :],
                                                       comb[:, bass.ds(q * SUB + s, 1), :].rearrange("p o e -> p (o e)")
                                                       .unsqueeze(2).to_broadcast([CH, NE, D]), ALU.mult))
                                link(vec.reduce_sum(red[s % 2][:, :], w[:, :, :].rearrange("p e d -> p d e"), axis=AX.X))
                                x = vec.tensor_tensor(res[r][:, s, :], red[s % 2][:, :],
                                                      h2[:, bass.ds(q * SUB + s, 1), :].rearrange("p o d -> p (o d)"), ALU.add)
                                if s == SUB - 1:
                                    x.then_inc(res_made, 1)


def arrange(inputs):
    import numpy as np
    g = {k: np.asarray(v) for k, v in inputs.items()}
    f = np.float32
    xf = g["x"].transpose(1, 0, 2).reshape(DIMS, TOK)
    xr = g["x"][:, :, ::-1].transpose(1, 0, 2).reshape(DIMS, TOK)
    ones = np.ones((3, TOK), f)
    z4, z64 = np.zeros((DIMS, D), f), np.zeros((D, D), f)
    w1, w2, w3, w4 = (g[f"L0_tok_W{k}"].T for k in (1, 2, 3, 4))
    b1, b2, b3, b4 = (g[f"L0_tok_b{k}"][None, :] for k in (1, 2, 3, 4))
    w, bias, wk = g["L0_attn_wqv_w"], g["L0_attn_wqv_b"], g["L0_attn_wk"]
    window = np.zeros((128, 62), f)
    window[0:64, 30] = 1.0
    window[64:128, 31] = 1.0
    select = np.zeros((6, 2, 128), f)
    vinit = np.zeros((128, 2, 2), f)
    for p in range(128):
        j, i, k = p // 32, (p % 32) // 2, p % 2
        for last in range(2):
            if not last or (i < LROWS and LROWS * j + i < LASTN):
                vinit[p, last, k] = 1.0
                if not on_scalar(i, j):
                    select[3 * k:3 * k + 3, last, p] = -0.5
    tri = np.zeros((NE, NE), f)
    for e in range(NE):
        tri[e, :e] = 1.0
    W1, W2 = g["L0_ffn_W1"], g["L0_ffn_W2"]
    return {
        "x10": np.concatenate([xf, xr, ones[0:2]]), "x7": np.concatenate([xf, ones]),
        "w1b": np.concatenate([np.concatenate([w1, z4], 1), np.concatenate([z4, w1], 1),
                               np.concatenate([b1, b1], 1), np.concatenate([b2, b2], 1)]),
        "w2b": np.concatenate([np.concatenate([w2, z64], 1), np.concatenate([z64, w2], 1)]),
        "w4d": np.concatenate([w4, w4]), "w3b": np.concatenate([w3, b3, b4, b4]),
        "ident": np.eye(128, dtype=f), "window": window, "select": select.reshape(6, 256), "vinit": vinit.reshape(128, 4),
        "wqv": np.concatenate([w.T, w.T]), "bq": bias[0:NH * D].reshape(HP, 128).T, "bv": bias[NH * D:],
        "wkc": wk.reshape(HP, 128).T, "wkt": wk.T,
        "fant": g["L0_attn_fanin_w"].T, "fb": g["L0_attn_fanin_b"],
        "wgt": g["L0_ffn_Wg"].T, "bg": g["L0_ffn_bg"], "tri": tri.reshape(-1),
        "w1t": np.concatenate([W1.transpose(2, 0, 1).reshape(D, NE * HID)] * 2),
        "b1c": g["L0_ffn_b1"].reshape(2 * NE, 128).T,
        "w2t": W2.reshape(NE, D, 2, 128).transpose(3, 0, 2, 1).reshape(128, NE * 2 * D),
        "b2": g["L0_ffn_b2"].reshape(-1),
    }


def kernel(**inputs):
    import numpy as np
    import concourse.bacc as _bacc
    from concourse.bass_utils import run_bass_kernel_spmd as _run

    nc = _bacc.Bacc("TRN2", target_bir_lowering=False, num_devices=1)
    arrays, aps = {}, {}
    for name, a in arrange(inputs).items():
        a = np.ascontiguousarray(a)
        arrays[f"in_{name}"] = a
        aps[name] = nc.dram_tensor(f"in_{name}", a.shape, F32, kind="ExternalInput").ap()
    out = nc.dram_tensor("out_h", (B, L, D), F32, kind="ExternalOutput").ap()
    build(nc, aps, out)
    r = _run(nc, [arrays], core_ids=[0])
    return r.results[0]["out_h"]
```
